# Optimizing a Trainium2 kernel written in Bass

```python
import numpy as np
import jax
import jax.numpy as jnp

def _softmax(x, axis=-1):
    return jax.nn.softmax(x, axis=axis)

def _gelu(x):
    return jax.nn.gelu(x, approximate=True)

def _silu(x):
    return jax.nn.silu(x)

def _sigmoid(x):
    return jax.nn.sigmoid(x)

def _layernorm(x, axis=-1, eps=1e-05):
    m = jnp.mean(x, axis=axis, keepdims=True)
    v = jnp.var(x, axis=axis, keepdims=True)
    return (x - m) / jnp.sqrt(v + eps)

def _scatter_add(tgt, idx, src, axis=0):
    return tgt.at[idx].add(src)

def _segment_sum(src, seg, n):
    return jax.ops.segment_sum(src, seg, n)
kernel_name = 'mk_adaln_d1_jaxref_r8_edb1f9'

def setup_inputs(seed: int=0):
    np.random.seed(seed)
    _w = jnp.asarray

    def _L0_attn_setup():
        import jax, jax.numpy as jnp
        import numpy as np
        D_INNER = 256
        D_STATE = 16
        DT_RANK = 128

        def _selective_ssm(x, A_log, D_param, x_proj_w, dt_proj_w, dt_proj_b):
            B, L, D = x.shape
            N = D_STATE
            x_dbl = jnp.einsum('bld,ed->ble', x, x_proj_w)
            dt, B_in, C_in = jnp.split(x_dbl, [DT_RANK, DT_RANK + N], axis=-1)
            delta = jax.nn.softplus(jnp.einsum('blr,dr->bld', dt, dt_proj_w) + dt_proj_b)
            A = -jnp.exp(A_log)
            xT = jnp.transpose(x, (1, 0, 2))
            dT = jnp.transpose(delta, (1, 0, 2))
            BT = jnp.transpose(B_in, (1, 0, 2))
            CT = jnp.transpose(C_in, (1, 0, 2))

            def step(h, inp):
                x_t, dt_t, B_t, C_t = inp
                dA = jnp.exp(dt_t[..., None] * A[None])
                dBx = dt_t[..., None] * B_t[:, None, :] * x_t[..., None]
                h = dA * h + dBx
                y_t = jnp.einsum('bdn,bn->bd', h, C_t) + D_param * x_t
                return (h, y_t)
            h0 = jnp.zeros((B, D, N), dtype=x.dtype)
            _, ys = jax.lax.scan(step, h0, (xT, dT, BT, CT))
            return jnp.transpose(ys, (1, 0, 2))
        key = jax.random.key(seed)
        k = jax.random.split(key, 6)
        B, L = (4, 512)
        x = jax.random.normal(k[0], (B, L, D_INNER), dtype=jnp.float32)
        A_log = jnp.log(jnp.broadcast_to(jnp.arange(1, D_STATE + 1, dtype=jnp.float32)[None, :], (D_INNER, D_STATE)))
        D_param = jnp.ones((D_INNER,), dtype=jnp.float32)
        fan_in = D_INNER
        bound = 1.0 / np.sqrt(fan_in)
        x_proj_w = jax.random.uniform(k[1], (DT_RANK + 2 * D_STATE, D_INNER), minval=-bound, maxval=bound, dtype=jnp.float32)
        bound2 = 1.0 / np.sqrt(DT_RANK)
        dt_proj_w = jax.random.uniform(k[2], (D_INNER, DT_RANK), minval=-bound2, maxval=bound2, dtype=jnp.float32)
        dt_init = jnp.exp(jax.random.uniform(k[3], (D_INNER,), dtype=jnp.float32) * (np.log(0.1) - np.log(0.001)) + np.log(0.001))
        dt_proj_b = jnp.log(jnp.exp(dt_init) - 1.0)
        return {'x': x, 'A_log': A_log, 'D_param': D_param, 'x_proj_w': x_proj_w, 'dt_proj_w': dt_proj_w, 'dt_proj_b': dt_proj_b}
    _L0_attn_in = _L0_attn_setup()

    def _L0_ffn_setup():
        import jax, jax.numpy as jnp
        import numpy as np
        HIDDEN = 256
        INTER = 704
        B, S = (2, 256)

        def _ternary(key, shape):
            return jax.random.randint(key, shape, -1, 2).astype(jnp.float32)
        key = jax.random.key(seed)
        ks = jax.random.split(key, 7)
        x = jax.random.normal(ks[0], (B, S, HIDDEN), dtype=jnp.float32)
        gate_w = _ternary(ks[1], (INTER, HIDDEN))
        up_w = _ternary(ks[2], (INTER, HIDDEN))
        down_w = _ternary(ks[3], (HIDDEN, INTER))
        gate_s = jax.random.uniform(ks[4], (INTER,), minval=0.01, maxval=0.1, dtype=jnp.float32)
        up_s = jax.random.uniform(ks[5], (INTER,), minval=0.01, maxval=0.1, dtype=jnp.float32)
        down_s = jax.random.uniform(ks[6], (HIDDEN,), minval=0.01, maxval=0.1, dtype=jnp.float32)
        return {'x': x, 'gate_w': gate_w, 'up_w': up_w, 'down_w': down_w, 'gate_s': gate_s, 'up_s': up_s, 'down_s': down_s}
    _L0_ffn_in = _L0_ffn_setup()
    _L0_c = _w((lambda *s: np.random.randn(*s).astype(np.float32) * 0.05)(1, 256))
    _L0_wmod = _w((lambda *s: np.random.randn(*s).astype(np.float32) * 0.05)(256, 6 * 256) * 256 ** (-0.5))
    _d = {'L0_attn_x': _L0_attn_in['x'], 'L0_attn_A_log': _L0_attn_in['A_log'], 'L0_attn_D_param': _L0_attn_in['D_param'], 'L0_attn_x_proj_w': _L0_attn_in['x_proj_w'], 'L0_attn_dt_proj_w': _L0_attn_in['dt_proj_w'], 'L0_attn_dt_proj_b': _L0_attn_in['dt_proj_b'], 'L0_ffn_gate_w': _L0_ffn_in['gate_w'], 'L0_ffn_up_w': _L0_ffn_in['up_w'], 'L0_ffn_down_w': _L0_ffn_in['down_w'], 'L0_ffn_gate_s': _L0_ffn_in['gate_s'], 'L0_ffn_up_s': _L0_ffn_in['up_s'], 'L0_ffn_down_s': _L0_ffn_in['down_s'], 'L0_c': _L0_c, 'L0_wmod': _L0_wmod}
    _x0 = _d['L0_attn_x']
    _d['L0_attn_x'] = jax.random.normal(jax.random.fold_in(jax.random.key(seed), 1), (1, 2048, 256), dtype=_x0.dtype)
    del _x0
    return _d

def reference(L0_attn_x, L0_attn_A_log, L0_attn_D_param, L0_attn_x_proj_w, L0_attn_dt_proj_w, L0_attn_dt_proj_b, L0_ffn_gate_w, L0_ffn_up_w, L0_ffn_down_w, L0_ffn_gate_s, L0_ffn_up_s, L0_ffn_down_s, L0_c, L0_wmod):

    def _L0_attn_ref(x, A_log, D_param, x_proj_w, dt_proj_w, dt_proj_b):
        import jax, jax.numpy as jnp
        import numpy as np
        D_INNER = 256
        D_STATE = 16
        DT_RANK = 128

        def _selective_ssm(x, A_log, D_param, x_proj_w, dt_proj_w, dt_proj_b):
            B, L, D = x.shape
            N = D_STATE
            x_dbl = jnp.einsum('bld,ed->ble', x, x_proj_w)
            dt, B_in, C_in = jnp.split(x_dbl, [DT_RANK, DT_RANK + N], axis=-1)
            delta = jax.nn.softplus(jnp.einsum('blr,dr->bld', dt, dt_proj_w) + dt_proj_b)
            A = -jnp.exp(A_log)
            xT = jnp.transpose(x, (1, 0, 2))
            dT = jnp.transpose(delta, (1, 0, 2))
            BT = jnp.transpose(B_in, (1, 0, 2))
            CT = jnp.transpose(C_in, (1, 0, 2))

            def step(h, inp):
                x_t, dt_t, B_t, C_t = inp
                dA = jnp.exp(dt_t[..., None] * A[None])
                dBx = dt_t[..., None] * B_t[:, None, :] * x_t[..., None]
                h = dA * h + dBx
                y_t = jnp.einsum('bdn,bn->bd', h, C_t) + D_param * x_t
                return (h, y_t)
            h0 = jnp.zeros((B, D, N), dtype=x.dtype)
            _, ys = jax.lax.scan(step, h0, (xT, dT, BT, CT))
            return jnp.transpose(ys, (1, 0, 2))
        return _selective_ssm(x, A_log, D_param, x_proj_w, dt_proj_w, dt_proj_b)

    def _L0_ffn_ref(x, gate_w, up_w, down_w, gate_s, up_s, down_s):
        import jax, jax.numpy as jnp
        import numpy as np
        HIDDEN = 256
        INTER = 704
        B, S = (2, 256)

        def _ternary(key, shape):
            return jax.random.randint(key, shape, -1, 2).astype(jnp.float32)
        b, s, h = x.shape
        xf = x.reshape(b * s, h)
        g = jnp.einsum('th,ih->ti', xf, gate_w) * gate_s
        u = jnp.einsum('th,ih->ti', xf, up_w) * up_s
        hdn = jax.nn.silu(g) * u
        out = jnp.einsum('ti,hi->th', hdn, down_w) * down_s
        return out.reshape(b, s, -1)
    x = L0_attn_x
    mod = (_silu(L0_c) @ L0_wmod).reshape(L0_c.shape[0], 6, 1, -1)
    sa, ca, ga, sb, cb, gb = (mod[:, 0], mod[:, 1], mod[:, 2], mod[:, 3], mod[:, 4], mod[:, 5])
    ga = (2 * (ga >= 0) - 1) * jnp.maximum(jnp.abs(ga), 0.25)
    gb = (2 * (gb >= 0) - 1) * jnp.maximum(jnp.abs(gb), 0.25)
    h = _layernorm(x, axis=-1) * (1 + ca) + sa
    x = x + ga * _L0_attn_ref(h, L0_attn_A_log, L0_attn_D_param, L0_attn_x_proj_w, L0_attn_dt_proj_w, L0_attn_dt_proj_b)
    h = _layernorm(x, axis=-1) * (1 + cb) + sb
    x = x + gb * _L0_ffn_ref(h, L0_ffn_gate_w, L0_ffn_up_w, L0_ffn_down_w, L0_ffn_gate_s, L0_ffn_up_s, L0_ffn_down_s)
    return x

_drawn_inputs = setup_inputs


def setup_inputs(seed=0):
    import zlib

    import numpy as np

    out = dict(_drawn_inputs(seed))
    spreads = {'L0_attn_D_param': (1.0, 0.2)}
    factors = {}
    for name, (base, spread) in spreads.items():
        noise = np.random.default_rng([zlib.crc32(name.encode()), seed]).standard_normal(out[name].shape)
        drawn = base * np.exp(spread * noise) if base else spread * noise
        out[name] = jnp.asarray(drawn.astype(out[name].dtype))
    for name, factor in factors.items():
        out[name] = (out[name] * factor).astype(out[name].dtype)
    return out
```

```python
import concourse.bass as bass
import concourse.mybir as mybir
from contextlib import ExitStack

F32 = mybir.dt.float32
ALU = mybir.AluOpType
ACT = mybir.ActivationFunctionType

P = 128
T = 2048
D = 256
HALVES = D // P
N = 16
R = 128
INTER = 704
FULL = INTER // P
REST = INTER - FULL * P
EPS = 1e-5
EXP_CAP = 1e17

CHUNK = [256, 512, 512, 512, 256]
NCH = len(CHUNK)
TOK0 = [sum(CHUNK[:c]) for c in range(NCH)]
NBLK = [s // P for s in CHUNK]
BLK0 = [t // P for t in TOK0]
NPAIR = [b // 2 for b in NBLK]
PAIR0 = [b // 2 for b in BLK0]

COL_ALOG = 0
COL_D = COL_ALOG + HALVES * N
COL_DTB = COL_D + HALVES
COL_GS = COL_DTB + HALVES
COL_US = COL_GS + FULL + 1
COL_C = COL_US + FULL
NPACK = COL_C + HALVES

PLAN = {
    "vector": {
        0: ["L hdn3", "L hdn4", "K stats"], 1: ["K nmr"], 2: ["F stats"], 3: ["L out0", "F nmr"], 5: ["L out1"],
        8: ["F cap"], 9: ["F delta"], 12: ["F dterm", "K hdn5"], 13: ["K hdn0"], 14: ["K hdn1"], 15: ["K hdn2"],
    },
    "gpsimd": {0: ["K rstd"], 2: ["F rstd"]},
    "scalar": {
        2: ["K xn"], 3: ["K h2", "K gate0"], 4: ["K gate1", "F xn"], 5: ["F hmod"],
        6: ["F dt", "K gate2"], 7: ["F bT"], 8: ["F exp"], 9: ["F ln", "K gate3"],
        11: ["F c", "K gate4", "K mixed", "K silu"],
    },
    "tensor": {
        0: ["L up4"], 1: ["L down0"], 2: ["L down1", "K h2T", "K gate0"], 3: ["L down2", "K gate1"],
        4: ["L down3", "F xT"], 5: ["F dt", "K gate2"], 6: ["F bT"], 7: ["F z"], 8: ["K gate3"],
        10: ["F c", "K gate4", "K mixed"], 11: ["F dterm"], 12: ["K up0"], 13: ["K up1"], 14: ["K up2"],
        15: ["K up3"],
    },
    "sync": {0: ["B 1"], 3: ["L out0"], 4: ["B 2"], 5: ["L out1"], 7: ["F bT"], 8: ["B 3"], 12: ["B 4"]},
}
FIRST_F = -1
LAST = NCH + 1


def side_tasks(engine, step, slot):
    for task in PLAN[engine].get(slot, []):
        kind, name = task.split(" ")
        chunk = {"F": step + 1, "K": step - 1, "L": step - 2}.get(kind, step)
        if 0 <= chunk < NCH:
            if name in ("down2", "down3", "out1") and NBLK[chunk] < 4:
                continue
            yield kind, name, chunk


def bank_uses():
    order = ["mod"]
    for step in range(FIRST_F, LAST + 1):
        for slot in range(N):
            for kind, name, c in side_tasks("tensor", step, slot):
                key = f"{kind} {name}".replace("L", "K")
                if key in ("F xT", "F z", "K h2T"):
                    order += [(key, c, h) for h in range(HALVES)]
                elif key == "F dterm":
                    order += [(key, c, q) for q in range(NPAIR[c])]
                elif name[:4] == "down":
                    blk = int(name[-1])
                    if blk % 2 == 0:
                        order.append(("K down", c, blk // 2))
                else:
                    order.append((key, c, 0))
        if step == FIRST_F:
            order.append("gb row")
    return {use: i for i, use in enumerate(order)}


def adaln_block(nc, x, wmod, pack, down_s, xprojT, dtprojT, gateT, upT, downT, out):
    USE = bank_uses()
    SIDE = 3
    RING_HT = 3
    RING_DRIVE = 3
    RING_B = 2
    GROUP = 4
    MAXC = max(CHUNK)

    ctx = ExitStack()
    with ctx:
        def sb(name, shape):
            return ctx.enter_context(nc.sbuf_tensor(name, shape, F32))

        def bank(name):
            return ctx.enter_context(nc.psum_tensor(name, [P, 512], F32))

        def sem(name):
            return ctx.enter_context(nc.semaphore(name))

        pack_sb = sb("pack_sb", [P, NPACK])
        xproj_sb = sb("xproj_sb", [P, HALVES, R + 2 * N])
        dtproj_sb = sb("dtproj_sb", [P, D])
        gate_sb = sb("gate_sb", [P, HALVES, INTER])
        up_sb = sb("up_sb", [P, HALVES, INTER])
        mixed_sb = sb("mixed_sb", [P, HALVES, 2 * REST])
        down_sb = sb("down_sb", [P, FULL + 1, D])
        gbds = sb("gbds", [P, D])
        ident = sb("ident", [P, P])
        A = sb("A", [P, HALVES * N])
        sigc = sb("sigc", [P, HALVES])
        silc = sb("silc", [P, HALVES])
        silc_wide = sb("silc_wide", [P, HALVES, P])
        mod = sb("mod", [P, 12])
        sgn = sb("sgn", [P, HALVES])
        ga = sb("ga", [P, HALVES])
        gaD = sb("gaD", [P, HALVES])
        diag_gaD = sb("diag_gaD", [P, HALVES, P])
        row_sgn = sb("row_sgn", [P, D])
        row_abs = sb("row_abs", [P, D])
        minus_half = sb("minus_half", [P, 4])
        resid = sb("resid", [P, T // P, D])
        stats = {k: sb(f"stats_{k}", [P, 4, 6]) for k in "FK"}
        meanvar = {k: sb(f"meanvar_{k}", [P, 4, 2]) for k in "FK"}
        vareps = {k: sb(f"vareps_{k}", [P, 4]) for k in "FK"}
        rstd = {k: sb(f"rstd_{k}", [P, 4]) for k in "FK"}
        nmr = {k: sb(f"nmr_{k}", [P, 4]) for k in "FK"}
        xn = {k: sb(f"xn_{k}", [P, 4, D]) for k in "FK"}
        hmod = sb("hmod", [P, HALVES, MAXC])
        dt_sb = sb("dt_sb", [P, MAXC])
        bT_sb = sb("bT_sb", [N, MAXC])
        C_sb = sb("C_sb", [P, 2, 4, N])
        splus = sb("splus", [P, HALVES, MAXC])
        delta = sb("delta", [P, 2, HALVES, MAXC])
        u = sb("u", [P, 2, HALVES, MAXC])
        brow = [sb(f"brow{i}", [P, GROUP, MAXC]) for i in range(RING_B)]
        drive = [sb(f"drive{i}", [P, HALVES, MAXC]) for i in range(RING_DRIVE)]
        state = sb("state", [P, N, HALVES, MAXC])
        wmod_sb = state[:, N - 3:N, :, :].rearrange("p n h t -> p (n h t)").rearrange("p (k e) -> p k e", k=HALVES)
        h2 = sb("h2", [P, HALVES, MAXC])
        gates = sb("gates", [P, 2, FULL + 1, MAXC])
        up5 = sb("up5", [P, MAXC])
        bT_dram = nc.dram_tensor("bT_dram", (N, T), F32, kind="Internal").ap()

        decay = [bank(f"decay{i}") for i in range(2)]
        stateT = [bank(f"stateT{i}") for i in range(RING_HT)]
        side = [bank(f"side{i}") for i in range(SIDE)]

        x_loaded = [sem(f"x_loaded{c}") for c in range(NCH)]
        pack_loaded = sem("pack_loaded")
        wmod_loaded = sem("wmod_loaded")
        proj_loaded = sem("proj_loaded")
        ffn_loaded = sem("ffn_loaded")
        down_loaded = sem("down_loaded")
        ident_ready = sem("ident_ready")
        minus_half_ready = sem("minus_half_ready")
        expc_ready = sem("expc_ready")
        silc_steps = sem("silc_steps")
        A_exp_ready = sem("A_exp_ready")
        A_ready = sem("A_ready")
        mod_steps = sem("mod_steps")
        clamp_steps = sem("clamp_steps")
        down_scaled = sem("down_scaled")
        side_full = [sem(f"side_full{i}") for i in range(SIDE)]
        side_free = [sem(f"side_free{i}") for i in range(SIDE)]
        decay_ready = sem("decay_ready")
        drive_ready = sem("drive_ready")
        scan_done = sem("scan_done")
        stateT_ready = sem("stateT_ready")
        acc_done = sem("acc_done")
        brow_loaded = [sem(f"brow_loaded{i}") for i in range(RING_B)]
        bT_stored = sem("bT_stored")
        stats_ready = {k: sem(f"stats_ready_{k}") for k in "FK"}
        meanvar_ready = {k: sem(f"meanvar_ready_{k}") for k in "FK"}
        vareps_ready = {k: sem(f"vareps_ready_{k}") for k in "FK"}
        rstd_ready = {k: sem(f"rstd_ready_{k}") for k in "FK"}
        nmr_ready = {k: sem(f"nmr_ready_{k}") for k in "FK"}
        xn_ready = {k: sem(f"xn_ready_{k}") for k in "FK"}
        spexp_ready = sem("spexp_ready")
        spcap_ready = sem("spcap_ready")
        spln_ready = sem("spln_ready")
        u_ready = sem("u_ready")
        silu_ready = sem("silu_ready")
        hdn5_ready = sem("hdn5_ready")
        out_stored = sem("out_stored")

        def upto_scan(c, n, h):
            return (c * N + n) * HALVES + h + 1

        def upto_drive(c, n):
            return c * N + n + 1

        def pair_no(c, n, q):
            return PAIR0[c] * N + n * NPAIR[c] + q

        def upto_acc(c, n, b):
            return BLK0[c] * N + n * NBLK[c] + b + 1

        def last_of_pair(number):
            return 2 * (number + 1)

        def side_bank(use):
            return side[USE[use] % SIDE], USE[use] % SIDE, USE[use] // SIDE

        def emptied(use):
            return side_free[USE[use] % SIDE], USE[use] // SIDE + 1

        block = ctx.enter_context(nc.Block())
        steps = range(FIRST_F, LAST + 1)
        x_dram = x.rearrange("(b p) d -> p b d", p=P)
        out_dram = out.rearrange("(b p) d -> p b d", p=P)

        @block.sync
        def _(sp):
            def load_x(c):
                b0, b1 = BLK0[c], BLK0[c] + NBLK[c]
                sp.dma_start(resid[:, b0:b1, :], x_dram[:, b0:b1, :]).then_inc(x_loaded[c], 16)

            def load_brow(group):
                c, g = divmod(group, N // GROUP)
                if g == 0:
                    sp.wait_ge(bT_stored, 16 * (c + 1))
                if group >= RING_B:
                    sp.wait_ge(drive_ready, GROUP * (group - RING_B + 1))
                rows = bT_dram[g * GROUP:(g + 1) * GROUP, TOK0[c]:TOK0[c] + CHUNK[c]]
                sp.dma_start(brow[group % RING_B][:, :, 0:CHUNK[c]], rows.partition_broadcast(P))\
                  .then_inc(brow_loaded[group % RING_B], 16)

            load_x(0)
            sp.dma_start(xproj_sb[:, :, :], xprojT.rearrange("(k p) e -> p k e", p=P)).then_inc(proj_loaded, 16)
            sp.dma_start(dtproj_sb[:, :], dtprojT).then_inc(proj_loaded, 16)
            for c in range(1, NCH):
                load_x(c)
            for step in steps:
                for slot in range(N):
                    for kind, name, c in side_tasks("sync", step, slot):
                        if kind == "B" and 0 <= step < NCH:
                            g = int(name)
                            if g < N // GROUP:
                                load_brow(step * (N // GROUP) + g)
                            elif step + 1 < NCH:
                                load_brow((step + 1) * (N // GROUP))
                        elif kind == "F":
                            sp.wait_ge(*emptied(("F bT", c, 0)))
                            sp.dma_start(bT_dram[:, TOK0[c]:TOK0[c] + CHUNK[c]], bT_sb[:, 0:CHUNK[c]])\
                              .then_inc(bT_stored, 16)
                        elif kind == "L":
                            q = int(name[-1])
                            sp.wait_ge(*emptied(("K down", c, q)))
                            b = BLK0[c] + 2 * q
                            sp.dma_start(out_dram[:, b:b + 2, :], resid[:, b:b + 2, :]).then_inc(out_stored, 16)
                if step == FIRST_F:
                    load_brow(0)
            sp.wait_ge(out_stored, 16 * sum(NPAIR))

        @block.gpsimd
        def _(pool):
            nc.gpsimd.memset(ident[:, :], 0.0).then_inc(ident_ready, 1)
            nc.gpsimd.memset(minus_half[:, :], -0.5).then_inc(minus_half_ready, 1)
            pool.wait_ge(ident_ready, 1)
            nc.gpsimd.affine_select(out=ident[:, :], in_=ident[:, :], compare_op=ALU.not_equal, fill=1.0,
                                    base=0, pattern=[[-1, P]], channel_multiplier=1).then_inc(ident_ready, 1)
            pool.wait_ge(minus_half_ready, 1)

            def side_work(kind, name, c):
                nb = NBLK[c]
                if name == "rstd":
                    pool.wait_ge(meanvar_ready[kind], c + 1)
                    nc.gpsimd.tensor_scalar(vareps[kind][:, 0:nb], meanvar[kind][:, 0:nb, 1], EPS, 1.0,
                                            ALU.add, ALU.mult).then_inc(vareps_ready[kind], 1)
                    pool.wait_ge(vareps_ready[kind], c + 1)
                    nc.gpsimd.tensor_tensor(rstd[kind][:, 0:nb], vareps[kind][:, 0:nb], minus_half[:, 0:nb],
                                            ALU.pow).then_inc(rstd_ready[kind], 1)

            for step in steps:
                if step == 0:
                    pool.wait_ge(down_loaded, 48)
                    pool.wait_ge(mod_steps, 5)
                    nc.gpsimd.tensor_tensor(down_sb[:, 0:FULL, :], down_sb[:, 0:FULL, :],
                                            gbds[:, :].unsqueeze(1).to_broadcast([P, FULL, D]),
                                            ALU.mult).then_inc(down_scaled, 1)
                    pool.wait_ge(down_scaled, 1)
                    nc.gpsimd.tensor_tensor(down_sb[REST:P, FULL, :], down_sb[REST:P, FULL, :],
                                            gbds[REST:P, :], ALU.mult).then_inc(down_scaled, 1)
                    pool.wait_ge(down_scaled, 2)
                for n in range(N):
                    if 0 <= step < NCH:
                        c, S, j = step, CHUNK[step], step * N + n
                        if n == 0:
                            pool.wait_ge(u_ready, c + 1)
                        if n % GROUP == 0:
                            group = j // GROUP
                            pool.wait_ge(brow_loaded[group % RING_B], 16 * (group // RING_B + 1))
                        if j >= RING_DRIVE:
                            pool.wait_ge(scan_done, HALVES * (j - RING_DRIVE + 1))
                        b = brow[(j // GROUP) % RING_B][:, n % GROUP, 0:S]
                        nc.gpsimd.tensor_tensor(drive[j % RING_DRIVE][:, :, 0:S], u[:, c % 2, :, 0:S],
                                                b.unsqueeze(1).to_broadcast([P, HALVES, S]),
                                                ALU.mult).then_inc(drive_ready, 1)
                    for task in side_tasks("gpsimd", step, n):
                        side_work(*task)

        @block.scalar
        def _(act):
            act.dma_start(pack_sb[:, :], pack).then_inc(pack_loaded, 16)
            wmod_v = wmod.rearrange("(k p) e -> p k e", p=P)
            act.dma_start(wmod_sb[:, :, 0:3 * D], wmod_v[:, :, 0:3 * D]).then_inc(wmod_loaded, 16)
            act.dma_start(wmod_sb[:, :, 3 * D:], wmod_v[:, :, 3 * D:]).then_inc(wmod_loaded, 16)
            act.dma_start(gate_sb[:, :, :], gateT.rearrange("(k p) i -> p k i", p=P)).then_inc(ffn_loaded, 16)
            act.dma_start(up_sb[:, :, :], upT.rearrange("(k p) i -> p k i", p=P)).then_inc(ffn_loaded, 16)
            for w, at in ((gateT, 0), (upT, REST)):
                act.dma_start(mixed_sb[:, :, at:at + REST],
                              w.rearrange("(k p) i -> p k i", p=P)[:, :, FULL * P:]).then_inc(ffn_loaded, 16)
            act.dma_start(gbds[:, :], down_s.partition_broadcast(P)).then_inc(down_loaded, 16)
            act.dma_start(down_sb[:, 0:FULL, :],
                          downT[0:FULL * P, :].rearrange("(j p) d -> p j d", p=P)).then_inc(down_loaded, 16)
            act.dma_start(down_sb[REST:P, FULL, :], downT[FULL * P:, :]).then_inc(down_loaded, 16)
            nc.scalar.preload_act_table_set("natural_log_exp_and_others")
            act.wait_ge(pack_loaded, 16)
            nc.scalar.activation(sigc[:, :], pack_sb[:, COL_C:COL_C + HALVES], ACT.Exp, scale=-1.0)\
              .then_inc(expc_ready, 1)
            nc.scalar.activation(A[:, :], pack_sb[:, COL_ALOG:COL_ALOG + HALVES * N], ACT.Exp)\
              .then_inc(A_exp_ready, 1)

            def side_work(kind, name, c):
                S, nb = CHUNK[c], NBLK[c]
                if name == "xn":
                    act.wait_ge(nmr_ready[kind], c + 1)
                    for b in range(nb):
                        ins = nc.scalar.activation(xn[kind][:, b, :], resid[:, BLK0[c] + b, :], ACT.Identity,
                                                   scale=rstd[kind][:, b:b + 1], bias=nmr[kind][:, b:b + 1])
                    ins.then_inc(xn_ready[kind], 1)
                elif name in ("hmod", "h2"):
                    if name == "hmod":
                        to, key, at = hmod, "F xT", 0
                        act.wait_ge(mod_steps, 2)
                        if c:
                            act.wait_ge(u_ready, c)
                            act.wait_ge(*emptied(("F dterm", c - 1, NPAIR[c - 1] - 1)))
                    else:
                        to, key, at = h2, "K h2T", 6
                    for h in range(HALVES):
                        src, i, k = side_bank((key, c, h))
                        act.wait_ge(side_full[i], k + 1)
                        nc.scalar.activation(to[:, h, 0:S], src[:, 0:S], ACT.Identity,
                                             scale=mod[:, at + 2 + h:at + 3 + h],
                                             bias=mod[:, at + h:at + h + 1]).then_inc(side_free[i], 1)
                elif kind == "F" and name in ("dt", "bT", "c"):
                    src, i, k = side_bank((f"F {name}", c, 0))
                    if name == "bT" and c:
                        act.wait_ge(bT_stored, 16 * c)
                    act.wait_ge(side_full[i], k + 1)
                    if name == "dt":
                        to, src = dt_sb[:, 0:S], src[:, 0:S]
                    elif name == "bT":
                        to, src = bT_sb[:, 0:S], src[0:N, 0:S]
                    else:
                        to, src = C_sb[:, c % 2, 0:nb, :], \
                            src[:, 0:nb * N].rearrange("p (b n) -> p b n", n=N)
                    nc.scalar.activation(to, src, ACT.Copy).then_inc(side_free[i], 1)
                elif name == "exp":
                    if c:
                        act.wait_ge(*emptied(("F z", c - 1, HALVES - 1)))
                    for h in range(HALVES):
                        src, i, k = side_bank(("F z", c, h))
                        act.wait_ge(side_full[i], k + 1)
                        nc.scalar.activation(splus[:, h, 0:S], src[:, 0:S], ACT.Exp,
                                             bias=pack_sb[:, COL_DTB + h:COL_DTB + h + 1]).then_inc(spexp_ready, 1)
                elif name == "ln":
                    act.wait_ge(spcap_ready, c + 1)
                    nc.scalar.activation(splus[:, :, 0:S], splus[:, :, 0:S], ACT.Ln, bias=1.0)\
                      .then_inc(spln_ready, 1)
                elif name[:4] == "gate":
                    j = int(name[4:])
                    src, i, k = side_bank((f"K {name}", c, 0))
                    act.wait_ge(side_full[i], k + 1)
                    nc.scalar.activation(gates[:, c % 2, j, 0:S], src[:, 0:S], ACT.Copy,
                                         scale=pack_sb[:, COL_GS + j:COL_GS + j + 1]).then_inc(side_free[i], 1)
                elif name == "mixed":
                    src, i, k = side_bank(("K mixed", c, 0))
                    act.wait_ge(side_full[i], k + 1)
                    nc.scalar.activation(gates[REST:P, c % 2, FULL, 0:S], src[0:REST, 0:S], ACT.Copy,
                                         scale=pack_sb[0:REST, COL_GS + FULL:COL_GS + FULL + 1])
                    nc.scalar.activation(up5[REST:P, 0:S], src[REST:P, 0:S], ACT.Copy,
                                         scale=pack_sb[REST:P, COL_GS + FULL:COL_GS + FULL + 1])\
                      .then_inc(side_free[i], 1)
                elif name == "silu":
                    for j in range(FULL):
                        act.wait_ge(*emptied((f"K gate{j}", c, 0)))
                    act.wait_ge(*emptied(("K mixed", c, 0)))
                    nc.scalar.activation(gates[:, c % 2, 0:FULL, 0:S], gates[:, c % 2, 0:FULL, 0:S], ACT.Silu)
                    nc.scalar.activation(gates[REST:P, c % 2, FULL, 0:S], gates[REST:P, c % 2, FULL, 0:S], ACT.Silu)\
                      .then_inc(silu_ready, 1)
                    nc.scalar.preload_act_table_set("natural_log_exp_and_others")

            for step in steps:
                if step == 0:
                    act.wait_ge(A_ready, 1)
                for n in range(N):
                    if 0 <= step < NCH:
                        c, S = step, CHUNK[step]
                        if n == 0:
                            act.wait_ge(*emptied(("F z", c, HALVES - 1)))
                        for h in range(HALVES):
                            i = upto_scan(c, n, h) - 1
                            if i >= 2:
                                act.wait_ge(scan_done, i - 1)
                            nc.scalar.activation(decay[i % 2][:, 0:S], delta[:, c % 2, h, 0:S], ACT.Exp,
                                                 scale=A[:, h * N + n:h * N + n + 1]).then_inc(decay_ready, 1)
                    for task in side_tasks("scalar", step, n):
                        side_work(*task)

        @block.vector
        def _(dve):
            dve.wait_ge(expc_ready, 1)
            nc.vector.tensor_scalar(sigc[:, :], sigc[:, :], 1.0, None, ALU.add).then_inc(silc_steps, 1)
            dve.wait_ge(silc_steps, 1)
            nc.vector.reciprocal(sigc[:, :], sigc[:, :]).then_inc(silc_steps, 1)
            dve.wait_ge(silc_steps, 2)
            nc.vector.tensor_tensor(silc[:, :], sigc[:, :], pack_sb[:, COL_C:COL_C + HALVES], ALU.mult)\
              .then_inc(silc_steps, 1)
            dve.wait_ge(silc_steps, 3)
            nc.vector.tensor_copy(silc_wide[:, :, :], silc[:, :].unsqueeze(2).to_broadcast([P, HALVES, P]))\
              .then_inc(silc_steps, 1)
            dve.wait_ge(A_exp_ready, 1)
            nc.vector.tensor_scalar(A[:, :], A[:, :], -1.0, None, ALU.mult).then_inc(A_ready, 1)

            def ln_stats(kind, c):
                for b in range(NBLK[c]):
                    ins = nc.vector.bn_stats(stats[kind][:, b, :], resid[:, BLK0[c] + b, :])
                ins.then_inc(stats_ready[kind], 1)
                dve.wait_ge(stats_ready[kind], c + 1)
                for b in range(NBLK[c]):
                    ins = nc.vector.bn_aggr(meanvar[kind][:, b, :], stats[kind][:, b, :])
                ins.then_inc(meanvar_ready[kind], 1)

            def side_work(kind, name, c):
                S, nb = CHUNK[c], NBLK[c]
                if name == "stats":
                    if kind == "F":
                        dve.wait_ge(x_loaded[c], 16)
                    else:
                        dve.wait_ge(acc_done, upto_acc(c, N - 1, nb - 1))
                    ln_stats(kind, c)
                elif name == "nmr":
                    dve.wait_ge(rstd_ready[kind], c + 1)
                    nc.vector.scalar_tensor_tensor(nmr[kind][:, 0:nb], meanvar[kind][:, 0:nb, 0], -1.0,
                                                   rstd[kind][:, 0:nb], ALU.mult, ALU.mult)\
                      .then_inc(nmr_ready[kind], 1)
                elif name == "cap":
                    dve.wait_ge(spexp_ready, HALVES * (c + 1))
                    nc.vector.tensor_scalar(splus[:, :, 0:S], splus[:, :, 0:S], EXP_CAP, None, ALU.min)\
                      .then_inc(spcap_ready, 1)
                elif name == "delta":
                    dve.wait_ge(spln_ready, c + 1)
                    for h in range(HALVES):
                        src, i, k = side_bank(("F z", c, h))
                        dve.wait_ge(side_full[i], k + 1)
                        nc.vector.scalar_tensor_tensor(delta[:, c % 2, h, 0:S], src[:, 0:S],
                                                       pack_sb[:, COL_DTB + h:COL_DTB + h + 1],
                                                       splus[:, h, 0:S], ALU.add, ALU.max)\
                          .then_inc(side_free[i], 1)
                    dve.wait_ge(side_free[i], k + 1)
                    dve.wait_ge(*emptied(("F xT", c, HALVES - 1)))
                    for h in range(HALVES):
                        ins = nc.vector.scalar_tensor_tensor(u[:, c % 2, h, 0:S], delta[:, c % 2, h, 0:S],
                                                             ga[:, h:h + 1], hmod[:, h, 0:S],
                                                             ALU.mult, ALU.mult)
                    ins.then_inc(u_ready, 1)
                elif name == "dterm":
                    for q in range(NPAIR[c]):
                        src, i, k = side_bank(("F dterm", c, q))
                        dve.wait_ge(side_full[i], k + 1)
                        b = BLK0[c] + 2 * q
                        nc.vector.tensor_tensor(resid[:, b:b + 2, :], resid[:, b:b + 2, :],
                                                src[:, :].rearrange("p (b d) -> p b d", b=2), ALU.add)\
                          .then_inc(side_free[i], 1)
                elif name == "hdn5":
                    dve.wait_ge(silu_ready, c + 1)
                    dve.wait_ge(*emptied(("K mixed", c, 0)))
                    g = gates[REST:P, c % 2, FULL, 0:CHUNK[c]]
                    nc.vector.tensor_tensor(g, g, up5[REST:P, 0:CHUNK[c]], ALU.mult).then_inc(hdn5_ready, 1)
                elif name[:3] == "hdn":
                    j = int(name[3:])
                    src, i, k = side_bank((f"K up{j}", c, 0))
                    dve.wait_ge(silu_ready, c + 1)
                    dve.wait_ge(side_full[i], k + 1)
                    nc.vector.scalar_tensor_tensor(gates[:, c % 2, j, 0:S], src[:, 0:S],
                                                   pack_sb[:, COL_US + j:COL_US + j + 1], gates[:, c % 2, j, 0:S],
                                                   ALU.mult, ALU.mult).then_inc(side_free[i], 1)
                elif name[:3] == "out":
                    q = int(name[3:])
                    src, i, k = side_bank(("K down", c, q))
                    dve.wait_ge(side_full[i], k + 1)
                    b = BLK0[c] + 2 * q
                    nc.vector.tensor_tensor(resid[:, b:b + 2, :], resid[:, b:b + 2, :],
                                            src[:, :].rearrange("p (b d) -> p b d", b=2), ALU.add)\
                      .then_inc(side_free[i], 1)

            def add_state(c, n):
                for b in range(NBLK[c]):
                    number = pair_no(c, n, b // 2)
                    if b % 2 == 0:
                        dve.wait_ge(stateT_ready, number + 1)
                    if n:
                        dve.wait_ge(acc_done, upto_acc(c, n - 1, b))
                    elif b == 0:
                        dve.wait_ge(*emptied(("F c", c, 0)))
                        dve.wait_ge(*emptied(("F dterm", c, NPAIR[c] - 1)))
                    row = resid[:, BLK0[c] + b, :]
                    nc.vector.scalar_tensor_tensor(row, stateT[number % RING_HT][:, (b % 2) * D:(b % 2 + 1) * D],
                                                   C_sb[:, c % 2, b, n:n + 1], row, ALU.mult, ALU.add)\
                      .then_inc(acc_done, 1)

            clamp_count = [0]

            def clamp_gate(sign, to, gate, read=None):
                def link(ins):
                    clamp_count[0] += 1
                    ins.then_inc(clamp_steps, 1)
                    dve.wait_ge(clamp_steps, clamp_count[0])

                link(nc.vector.tensor_scalar(sign[:, :], gate, 0.0, 2.0, ALU.is_ge, ALU.mult))
                link(nc.vector.tensor_scalar(sign[:, :], sign[:, :], -1.0, None, ALU.add))
                link(nc.vector.tensor_tensor(to[:, :], gate, sign[:, :], ALU.mult))
                ins = nc.vector.scalar_tensor_tensor(to[:, :], to[:, :], 0.25, sign[:, :], ALU.max, ALU.mult)
                if read is None:
                    link(ins)
                else:
                    ins.then_inc(read, 1)
                    dve.wait_ge(*emptied("gb row"))

            def setup_mod():
                src, i, k = side_bank("mod")
                dve.wait_ge(side_full[i], k + 1)
                nc.vector.tensor_copy(mod[:, :], src[:, 0:12]).then_inc(side_free[i], 1)
                dve.wait_ge(side_free[i], k + 1)
                nc.vector.tensor_scalar(mod[:, 2:4], mod[:, 2:4], 1.0, None, ALU.add).then_inc(mod_steps, 1)
                nc.vector.tensor_scalar(mod[:, 8:10], mod[:, 8:10], 1.0, None, ALU.add).then_inc(mod_steps, 1)
                clamp_gate(sgn, ga, mod[:, 4:6])
                nc.vector.tensor_tensor(gaD[:, :], ga[:, :], pack_sb[:, COL_D:COL_D + HALVES], ALU.mult)\
                  .then_inc(mod_steps, 1)
                dve.wait_ge(mod_steps, 3)
                dve.wait_ge(ident_ready, 2)
                for h in range(HALVES):
                    ins = nc.vector.tensor_scalar(diag_gaD[:, h, :], ident[:, :], gaD[:, h:h + 1], None, ALU.mult)
                ins.then_inc(mod_steps, 1)

            def setup_gb():
                src, i, k = side_bank("gb row")
                dve.wait_ge(side_full[i], k + 1)
                clamp_gate(row_sgn, row_abs, src[:, 0:D], side_free[i])
                dve.wait_ge(down_loaded, 48)
                nc.vector.tensor_tensor(gbds[:, :], gbds[:, :], row_abs[:, :], ALU.mult).then_inc(mod_steps, 1)

            for step in steps:
                for n in range(N):
                    if 0 <= step < NCH:
                        c, S = step, CHUNK[step]
                        for h in range(HALVES):
                            i = upto_scan(c, n, h) - 1
                            dve.wait_ge(decay_ready, i + 1)
                            if h == 0:
                                dve.wait_ge(drive_ready, upto_drive(c, n))
                            before = state[:, n, h, CHUNK[c - 1] - 1:CHUNK[c - 1]] if c else 0.0
                            nc.vector.tensor_tensor_scan(state[:, n, h, 0:S], decay[i % 2][:, 0:S],
                                                         drive[(c * N + n) % RING_DRIVE][:, h, 0:S], before,
                                                         ALU.mult, ALU.add).then_inc(scan_done, 1)
                        if n:
                            add_state(c, n - 1)
                        elif c:
                            add_state(c - 1, N - 1)
                    elif step == NCH and n == 0:
                        add_state(NCH - 1, N - 1)
                    for task in side_tasks("vector", step, n):
                        side_work(*task)
                    if step == FIRST_F and n == 3:
                        setup_mod()
                if step == FIRST_F:
                    setup_gb()

        @block.tensor
        def _(pe):
            def take(use):
                to, i, k = side_bank(use)
                if k:
                    pe.wait_ge(side_free[i], k)
                return to, side_full[i]

            pe.wait_ge(wmod_loaded, 32)
            pe.wait_ge(silc_steps, 4)
            to, full = take("mod")
            for col in range(12):
                for k in range(HALVES):
                    ins = nc.tensor.matmul(to[:, col:col + 1], wmod_sb[:, k, col * P:(col + 1) * P],
                                           silc[:, k:k + 1], start=k == 0, stop=k == HALVES - 1)
            ins.then_inc(full, 1)
            pe.wait_ge(ident_ready, 2)

            def product(use, S, M, weights, data):
                to, full = take(use)
                for k in range(HALVES):
                    ins = nc.tensor.matmul(to[0:M, 0:S], weights(k), data(k), start=k == 0, stop=k == HALVES - 1)
                ins.then_inc(full, 1)

            def side_work(kind, name, c):
                S, nb = CHUNK[c], NBLK[c]
                if name in ("xT", "h2T"):
                    pe.wait_ge(xn_ready[kind], c + 1)
                    for h in range(HALVES):
                        to, full = take((f"{kind} {name}", c, h))
                        for b in range(nb):
                            ins = nc.tensor.transpose(to[:, b * P:(b + 1) * P],
                                                      xn[kind][:, b, h * P:(h + 1) * P], ident[:, :])
                        ins.then_inc(full, 1)
                elif name == "dt":
                    pe.wait_ge(proj_loaded, 32)
                    pe.wait_ge(*emptied(("F xT", c, HALVES - 1)))
                    product(("F dt", c, 0), S, R, lambda k: xproj_sb[:, k, 0:R], lambda k: hmod[:, k, 0:S])
                elif name == "bT":
                    product(("F bT", c, 0), S, N, lambda k: xproj_sb[:, k, R:R + N], lambda k: hmod[:, k, 0:S])
                elif name == "c":
                    to, full = take(("F c", c, 0))
                    for b in range(nb):
                        for k in range(HALVES):
                            ins = nc.tensor.matmul(to[:, b * N:(b + 1) * N], hmod[:, k, b * P:(b + 1) * P],
                                                   xproj_sb[:, k, R + N:R + 2 * N],
                                                   start=k == 0, stop=k == HALVES - 1)
                    ins.then_inc(full, 1)
                elif name == "z":
                    pe.wait_ge(*emptied(("F dt", c, 0)))
                    for h in range(HALVES):
                        to, full = take(("F z", c, h))
                        nc.tensor.matmul(to[:, 0:S], dtproj_sb[:, h * P:(h + 1) * P], dt_sb[:, 0:S],
                                         start=True, stop=True).then_inc(full, 1)
                elif name == "dterm":
                    pe.wait_ge(mod_steps, 4)
                    for q in range(NPAIR[c]):
                        to, full = take(("F dterm", c, q))
                        for b in range(2):
                            for h in range(HALVES):
                                ins = nc.tensor.matmul(to[:, b * D + h * P:b * D + (h + 1) * P],
                                                       hmod[:, h, (2 * q + b) * P:(2 * q + b + 1) * P],
                                                       diag_gaD[:, h, :], start=True, stop=True)
                        ins.then_inc(full, 1)
                elif name[:4] == "gate" or name[:2] == "up":
                    w, j = (gate_sb, int(name[4:])) if name[0] == "g" else (up_sb, int(name[2:]))
                    pe.wait_ge(ffn_loaded, 64)
                    pe.wait_ge(*emptied(("K h2T", c, HALVES - 1)))
                    product((f"K {name}", c, 0), S, P, lambda k: w[:, k, j * P:(j + 1) * P],
                            lambda k: h2[:, k, 0:S])
                elif name == "mixed":
                    product(("K mixed", c, 0), S, P, lambda k: mixed_sb[:, k, :], lambda k: h2[:, k, 0:S])
                elif name[:4] == "down":
                    b = int(name[4:])
                    if b == 0:
                        pe.wait_ge(down_scaled, 2)
                        pe.wait_ge(*emptied((f"K up{FULL - 1}", c, 0)))
                        pe.wait_ge(hdn5_ready, c + 1)
                    to, i, k = side_bank(("K down", c, b // 2))
                    if b % 2 == 0 and k:
                        pe.wait_ge(side_free[i], k)
                    rows = slice(b * P, (b + 1) * P)
                    to = to[:, (b % 2) * D:(b % 2 + 1) * D]
                    for j in range(FULL):
                        nc.tensor.matmul(to, gates[:, c % 2, j, rows], down_sb[:, j, :], start=j == 0, stop=False)
                    ins = nc.tensor.matmul(to, gates[REST:P, c % 2, FULL, rows], down_sb[REST:P, FULL, :],
                                           start=False, stop=True)
                    if b % 2:
                        ins.then_inc(side_full[i], 1)

            for step in steps:
                for n in range(N):
                    if 0 <= step < NCH:
                        c = step
                        pe.wait_ge(scan_done, upto_scan(c, n, HALVES - 1))
                        for q in range(NPAIR[c]):
                            number = pair_no(c, n, q)
                            if number >= RING_HT:
                                pe.wait_ge(acc_done, last_of_pair(number - RING_HT))
                            to = stateT[number % RING_HT]
                            for b in range(2):
                                for h in range(HALVES):
                                    ins = nc.tensor.transpose(
                                        to[:, b * D + h * P:b * D + (h + 1) * P],
                                        state[:, n, h, (2 * q + b) * P:(2 * q + b + 1) * P], ident[:, :])
                            ins.then_inc(stateT_ready, 1)
                    for task in side_tasks("tensor", step, n):
                        side_work(*task)
                if step == FIRST_F:
                    to, full = take("gb row")
                    for k in range(HALVES):
                        ins = nc.tensor.matmul(to[:, 0:D], silc_wide[:, k, :], wmod_sb[:, k, 5 * D:6 * D],
                                               start=k == 0, stop=k == HALVES - 1)
                    ins.then_inc(full, 1)


def kernel(L0_attn_x, L0_attn_A_log, L0_attn_D_param, L0_attn_x_proj_w, L0_attn_dt_proj_w, L0_attn_dt_proj_b,
           L0_ffn_gate_w, L0_ffn_up_w, L0_ffn_down_w, L0_ffn_gate_s, L0_ffn_up_s, L0_ffn_down_s, L0_c, L0_wmod):
    import numpy as np
    import concourse.bacc as bacc
    from concourse.bass_utils import run_bass_kernel_spmd

    def cols(v):
        return np.asarray(v).reshape(-1, P).T

    gate_s, up_s = np.asarray(L0_ffn_gate_s), np.asarray(L0_ffn_up_s)
    whole = FULL * P
    pack = np.concatenate([
        np.asarray(L0_attn_A_log).reshape(HALVES, P, N).transpose(1, 0, 2).reshape(P, HALVES * N),
        cols(L0_attn_D_param), cols(L0_attn_dt_proj_b),
        cols(gate_s[:whole]), np.concatenate([gate_s[whole:], up_s[whole:]])[:, None], cols(up_s[:whole]),
        cols(np.asarray(L0_c)[0]),
    ], axis=1)
    arrays = {
        "x": np.asarray(L0_attn_x)[0],
        "wmod": np.asarray(L0_wmod),
        "pack": pack,
        "down_s": np.asarray(L0_ffn_down_s),
        "xprojT": np.asarray(L0_attn_x_proj_w).T,
        "dtprojT": np.asarray(L0_attn_dt_proj_w).T,
        "gateT": np.asarray(L0_ffn_gate_w).T,
        "upT": np.asarray(L0_ffn_up_w).T,
        "downT": np.asarray(L0_ffn_down_w).T,
    }
    arrays = {k: np.ascontiguousarray(v) for k, v in arrays.items()}
    nc = bacc.Bacc("TRN2", target_bir_lowering=False, num_devices=1)
    args = [nc.dram_tensor(f"in_{k}", v.shape, mybir.dt.from_np(v.dtype), kind="ExternalInput").ap()
            for k, v in arrays.items()]
    out = nc.dram_tensor("out_0", (T, D), F32, kind="ExternalOutput").ap()
    adaln_block(nc, *args, out)
    r = run_bass_kernel_spmd(nc, [{f"in_{k}": v for k, v in arrays.items()}], core_ids=[0])
    return r.results[0]["out_0"].reshape(1, T, D)
```

```python
import concourse.bass as bass
import concourse.mybir as mybir
from contextlib import ExitStack

F32 = mybir.dt.float32
F32R = mybir.dt.float32r
I32 = mybir.dt.int32
ALU = mybir.AluOpType
ACT = mybir.ActivationFunctionType

P = 128
T = 2048
D = 256
HALVES = D // P
N = 16
R = 128
INTER = 704
FULL = INTER // P
REST = INTER - FULL * P
EPS = 1e-5
EXP_CAP = 1e17

CHUNK = [512, 512, 512, 512]
NCH = len(CHUNK)
TOK0 = [sum(CHUNK[:c]) for c in range(NCH)]
NBLK = [s // P for s in CHUNK]
BLK0 = [t // P for t in TOK0]
NPAIR = [b // 2 for b in NBLK]
PAIR0 = [b // 2 for b in BLK0]

COL_ALOG = 0
COL_D = COL_ALOG + HALVES * N
COL_DTB = COL_D + HALVES
COL_GS = COL_DTB + HALVES
COL_US = COL_GS + FULL + 1
COL_C = COL_US + FULL
NPACK = COL_C + HALVES

PLAN = {
    "vector": [
        (0, "K acc2"), (0, "F stats"), (0, "K stats"), (1, "F nmr"), (1, "K nmr"), (18, "K out0"),
        (20, "K out1"), (8, "F cap"), (9, "F delta"), (12, "F dterm"), (12, "K hdn5"), (13, "K hdn1"),
        (13, "K hdn0"), (14, "K hdn2"), (15, "K hdn3"), (15, "K hdn4"),
    ],
    "gpsimd": [
        (2, "F rstd"), (2, "K rstd"), (5, "K lo"),
    ],
    "scalar": [
        (2, "K xn0"), (3, "K xn1"), (3, "K h2hi"), (3, "K h2"), (4, "F xn0"), (5, "F xn1"),
        (5, "K gate2"), (6, "F hmod"), (6, "K gate1"), (7, "K gate0"), (7, "F dt"), (7, "K gate4"),
        (7, "F bT"), (8, "F exp"), (9, "F ln"), (9, "F c"), (10, "K mixed"), (11, "K gate3"),
        (12, "K silu"),
    ],
    "tensor": [
        (16, "K down1"), (16, "K down2"), (2, "K h2T"), (19, "K down3"), (3, "K gate2"), (4, "K gate1"),
        (4, "F xT"), (4, "K gate0"), (5, "F dt"), (5, "K gate4"), (6, "F bT"), (7, "F z"), (7, "K gate3"),
        (8, "F c"), (9, "K mixed"), (9, "K up0"), (10, "F dterm"), (12, "K up1"), (13, "K up2"),
        (13, "K up3"), (14, "K up4"), (15, "K down0"),
    ],
    "sync": [
        (0, "B 1"), (1, "B 2"), (18, "K out1"), (19, "K out0"), (6, "F bT"), (7, "B 3"), (13, "B 4"),
    ],
}
FIRST = {
    "vector": [
        (0, "F stats"), (4, "F nmr"), (4, "S mod"), (4, "F cap"), (8, "F delta"), (15, "F dterm"),
        (15, "S mod2"), (19, "S gb"), (20, "S equal"), (31, "S same"),
    ],
    "gpsimd": [
        (5, "F rstd"), (23, "S down"),
    ],
    "scalar": [
        (0, "F xn0"), (0, "F xn1"), (3, "F hmod"), (5, "F dt"), (6, "F bT"), (6, "F exp"), (10, "F c"),
        (12, "F ln"), (18, "S hi0"), (20, "S hi1"), (22, "S same0"), (23, "S same1"),
    ],
    "tensor": [
        (0, "S warm"), (0, "S warm"), (0, "S warm"), (1, "S mod"), (2, "F xT"), (2, "S warm"),
        (2, "F dt"), (4, "F bT"), (6, "F z"), (12, "F c"), (13, "F dterm"), (15, "S mod2"), (18, "S gb"),
        (29, "S same"),
    ],
    "sync": [
        (6, "F bT"), (6, "B 0"), (7, "S wmod"), (8, "S x"), (10, "S ffn"), (11, "S down"),
    ],
}
FINAL = {
    "vector": [
        (0, "K acc2"), (1, "K stats"), (2, "K nmr"), (3, "K h2"), (3, "K lo"), (4, "K hdn0"),
        (6, "K hdn5"), (6, "K hdn1"), (7, "K hdn2"), (8, "K hdn3"), (9, "K hdn4"), (9, "K out0"),
        (10, "K out1"),
    ],
    "gpsimd": [
        (3, "K rstd"),
    ],
    "scalar": [
        (0, "K xn0"), (1, "K xn1"), (2, "K h2hi"), (3, "K mixed"), (4, "K gate0"), (5, "K gate4"),
        (5, "K gate1"), (8, "K gate2"), (8, "K gate3"),
    ],
    "tensor": [
        (2, "K h2T"), (4, "K mixed"), (4, "K gate0"), (4, "K up0"), (6, "K gate4"), (7, "K gate1"),
        (7, "K up1"), (7, "K gate2"), (7, "K up2"), (7, "K gate3"), (7, "K up3"), (7, "K up4"),
        (8, "K down0"), (9, "K down2"),
    ],
    "sync": [
        (8, "K out0"), (10, "K out1"),
    ],
}
ACT_STATES = [0, 8, 12, 14]
KEEP_LAG = 2
MUL_LAG = 1
SUM_LAG = 3
SIDE = 4
RING_HT = 2
WARM_UP = 24
KEEP_WARM = 5
RING_STATE = 6
RING_B = 2
GROUP = 4
RING_DECAY = 2
FIRST_F = -1
LAST = NCH + 1


def side_tasks(engine, step, slot):
    for plan in (PLAN, FIRST, FINAL):
        for at, task in plan[engine]:
            if at % N != slot:
                continue
            kind, name = task.split(" ")
            if plan is FIRST:
                chunk = step - FIRST_F - at // N
                if chunk != 0:
                    continue
            else:
                chunk = step - at // N + {"F": 1, "K": -1, "B": 0}[kind]
                if not 0 <= chunk < NCH or (kind, chunk) == ("F", 0) or \
                        kind == "K" and (chunk == NCH - 1) != (plan is FINAL):
                    continue
            if name in ("down2", "down3", "out1", "xn1") and NBLK[chunk] < 4:
                continue
            yield kind, name, chunk


def lagged(step, slot, lag):
    j = step * N + slot - lag
    return [divmod(j, N)] if 0 <= j < NCH * N else []


def bank_uses():
    order = []
    for step in range(FIRST_F, LAST + 1):
        for slot in range(N):
            for kind, name, c in side_tasks("tensor", step, slot):
                key = f"{kind} {name}"
                if key in ("F xT", "F z", "K h2T"):
                    order += [(key, c, h) for h in range(HALVES)]
                elif key == "F dterm":
                    order += [(key, c, q) for q in range(NPAIR[c])]
                elif name[:4] == "down":
                    blk = int(name[-1])
                    if blk % 2 == 0:
                        order.append(("K down", c, blk // 2))
                elif name != "warm":
                    order.append((key, c, 0))
    return {use: i for i, use in enumerate(order)}


def adaln_block(nc, x, wmod, pack, down_s, xprojT, dtprojT, gateT, upT, downT, out):
    USE = bank_uses()
    MAXC = max(CHUNK)

    ctx = ExitStack()
    with ctx:
        def sb(name, shape, dtype=F32):
            return ctx.enter_context(nc.sbuf_tensor(name, shape, dtype))

        def bank(name):
            return ctx.enter_context(nc.psum_tensor(name, [P, 512], F32))

        def sem(name):
            return ctx.enter_context(nc.semaphore(name))

        wmod_sb = sb("wmod_sb", [P, HALVES, 6 * D])
        pack_sb = sb("pack_sb", [P, NPACK])
        xproj_sb = sb("xproj_sb", [P, HALVES, R + 2 * N])
        dtproj_sb = sb("dtproj_sb", [P, D])
        ffn_sb = sb("ffn_sb", [P, HALVES, 2 * INTER])
        ffn_hi = sb("ffn_hi", [P, HALVES, 2 * INTER], F32R)
        same = sb("same", [P, HALVES])
        ones = sb("ones", [P, 1])
        needs_full = sb("needs_full", [1, 1], I32)
        down_sb = sb("down_sb", [P, FULL + 1, D])
        gbds = sb("gbds", [P, D])
        ident = sb("ident", [P, P])
        A = sb("A", [P, HALVES * N])
        sigc = sb("sigc", [P, HALVES])
        silc = sb("silc", [P, HALVES])
        silc_wide = sb("silc_wide", [P, HALVES, P])
        mod = sb("mod", [P, 12])
        sgn = sb("sgn", [P, HALVES])
        ga = sb("ga", [P, HALVES])
        gaD = sb("gaD", [P, HALVES])
        diag_gaD = sb("diag_gaD", [P, HALVES, P])
        row_sgn = sb("row_sgn", [P, D])
        row_abs = sb("row_abs", [P, D])
        minus_half = sb("minus_half", [P, 4])
        resid = sb("resid", [P, T // P, D])
        stats = {k: sb(f"stats_{k}", [P, 4, 6]) for k in "FK"}
        meanvar = {k: sb(f"meanvar_{k}", [P, 4, 2]) for k in "FK"}
        vareps = {k: sb(f"vareps_{k}", [P, 4]) for k in "FK"}
        rstd = {k: sb(f"rstd_{k}", [P, 4]) for k in "FK"}
        nmr = {k: sb(f"nmr_{k}", [P, 4]) for k in "FK"}
        xn = {k: sb(f"xn_{k}", [P, 4, D]) for k in "FK"}
        hmod = sb("hmod", [P, HALVES, MAXC])
        dt_sb = sb("dt_sb", [P, MAXC])
        bT_sb = sb("bT_sb", [N, MAXC])
        C_sb = sb("C_sb", [P, 2, 4, N])
        splus = sb("splus", [P, HALVES, MAXC])
        delta = sb("delta", [P, 2, HALVES, MAXC])
        u = sb("u", [P, 2, HALVES, MAXC])
        brow = [sb(f"brow{i}", [P, GROUP, MAXC]) for i in range(RING_B)]
        state = [sb(f"state{i}", [P, HALVES, MAXC]) for i in range(RING_STATE)]
        last = sb("last", [P, N, HALVES])
        acc2 = sb("acc2", [P, 4, D])
        prod = [sb(f"prod{i}", [P, 4, D]) for i in range(2)]
        h2 = sb("h2", [P, HALVES, MAXC])
        h2_hi = sb("h2_hi", [P, HALVES, MAXC], F32R)
        h2_lo = sb("h2_lo", [P, HALVES, MAXC], F32R)
        gates = sb("gates", [P, 2, FULL + 1, MAXC])
        up5 = sb("up5", [P, MAXC])
        bT_dram = nc.dram_tensor("bT_dram", (N, T), F32, kind="Internal").ap()

        decay = [bank(f"decay{i}") for i in range(RING_DECAY)]
        stateT = [bank(f"stateT{i}") for i in range(RING_HT)]
        side = [bank(f"side{i}") for i in range(SIDE)]

        x_loaded = [sem(f"x_loaded{c}") for c in range(NCH)]
        pack_loaded = sem("pack_loaded")
        wmod_loaded = sem("wmod_loaded")
        wmod2_loaded = sem("wmod2_loaded")
        proj_loaded = sem("proj_loaded")
        ffn_loaded = sem("ffn_loaded")
        down_loaded = sem("down_loaded")
        ident_ready = sem("ident_ready")
        minus_half_ready = sem("minus_half_ready")
        expc_ready = sem("expc_ready")
        silc_steps = sem("silc_steps")
        A_exp_ready = sem("A_exp_ready")
        A_ready = sem("A_ready")
        mod_steps = sem("mod_steps")
        gbds_ready = sem("gbds_ready")
        clamp_steps = sem("clamp_steps")
        down_scaled = sem("down_scaled")
        side_full = [sem(f"side_full{i}") for i in range(SIDE)]
        side_free = [sem(f"side_free{i}") for i in range(SIDE)]
        decay_ready = sem("decay_ready")
        drive_ready = sem("drive_ready")
        scan_done = sem("scan_done")
        last_kept = sem("last_kept")
        prod_ready = sem("prod_ready")
        acc2_ready = sem("acc2_ready")
        acc2_added = sem("acc2_added")
        h2_lo_ready = sem("h2_lo_ready")
        h2_hi_ready = sem("h2_hi_ready")
        ffn_hi_ready = sem("ffn_hi_ready")
        equal_ready = sem("equal_ready")
        same_ready = sem("same_ready")
        ones_ready = sem("ones_ready")
        stateT_ready = sem("stateT_ready")
        acc_done = sem("acc_done")
        brow_loaded = [sem(f"brow_loaded{i}") for i in range(RING_B)]
        bT_stored = sem("bT_stored")
        stats_ready = {k: sem(f"stats_ready_{k}") for k in "FK"}
        meanvar_ready = {k: sem(f"meanvar_ready_{k}") for k in "FK"}
        vareps_ready = {k: sem(f"vareps_ready_{k}") for k in "FK"}
        rstd_ready = {k: sem(f"rstd_ready_{k}") for k in "FK"}
        nmr_ready = {k: sem(f"nmr_ready_{k}") for k in "FK"}
        xn_ready = {k: sem(f"xn_ready_{k}") for k in "FK"}
        spexp_ready = sem("spexp_ready")
        spcap_ready = sem("spcap_ready")
        spln_ready = sem("spln_ready")
        u_ready = sem("u_ready")
        silu_ready = sem("silu_ready")
        hdn5_ready = sem("hdn5_ready")
        out_stored = sem("out_stored")

        def upto_scan(c, n, h):
            return (c * N + n) * HALVES + h + 1

        def upto_drive(c, n):
            return c * N + n + 1

        def pair_no(c, n, q):
            return PAIR0[c] * N + n * NPAIR[c] + q

        def dve_states(n):
            return n + 1 - sum(m <= n for m in ACT_STATES)

        def upto_acc(c, n, b):
            return BLK0[c] * dve_states(N - 1) + (dve_states(n) - 1) * NBLK[c] + b + 1

        def upto_prod(c, n, q=-1):
            return PAIR0[c] * len(ACT_STATES) + ACT_STATES.index(n) * NPAIR[c] + q % NPAIR[c] + 1

        def upto_acc2(c, n):
            return c * (len(ACT_STATES) - 1) + ACT_STATES.index(n)

        def pair_read(c, n, q):
            if n in ACT_STATES:
                return prod_ready, upto_prod(c, n, q)
            return acc_done, upto_acc(c, n, 2 * q + 1)

        PAIRS = [(c, n, q) for c in range(NCH) for n in range(N) for q in range(NPAIR[c])]

        def side_bank(use):
            return side[USE[use] % SIDE], USE[use] % SIDE, USE[use] // SIDE

        def emptied(use):
            return side_free[USE[use] % SIDE], USE[use] // SIDE + 1

        block = ctx.enter_context(nc.Block())
        steps = range(FIRST_F, LAST + 1)
        wmod_v = wmod.rearrange("(k p) e -> p k e", p=P)
        x_dram = x.rearrange("(b p) d -> p b d", p=P)
        out_dram = out.rearrange("(b p) d -> p b d", p=P)

        def low_part(engine, c):
            S = CHUNK[c]
            engine.wait_ge(*emptied(("K h2T", c, HALVES - 1)))
            engine.tensor_tensor(h2_lo[:, :, 0:S], h2[:, :, 0:S], h2_hi[:, :, 0:S].bitcast(F32),
                                 ALU.subtract).then_inc(h2_lo_ready, 1)

        gates_flat = gates[:, :, :, :].rearrange("p a j t -> p (a j t)")[:, 0:2 * HALVES * INTER]\
            .rearrange("p (k i) -> p k i", k=HALVES)

        @block.sync
        def _(sp):
            def load_x(c):
                b0, b1 = BLK0[c], BLK0[c] + NBLK[c]
                sp.dma_start(resid[:, b0:b1, :], x_dram[:, b0:b1, :]).then_inc(x_loaded[c], 16)

            def load_brow(group):
                c, g = divmod(group, N // GROUP)
                if g == 0:
                    sp.wait_ge(bT_stored, 16 * (c + 1))
                if group >= RING_B:
                    sp.wait_ge(drive_ready, GROUP * (group - RING_B + 1))
                rows = bT_dram[g * GROUP:(g + 1) * GROUP, TOK0[c]:TOK0[c] + CHUNK[c]]
                sp.dma_start(brow[group % RING_B][:, :, 0:CHUNK[c]], rows.partition_broadcast(P))\
                  .then_inc(brow_loaded[group % RING_B], 16)

            def load_more(name):
                if name == "wmod":
                    sp.dma_start(wmod_sb[:, :, 3 * D:], wmod_v[:, :, 3 * D:]).then_inc(wmod2_loaded, 16)
                elif name == "x":
                    for c in range(1, NCH):
                        load_x(c)
                elif name == "ffn":
                    for m, w in enumerate((gateT, upT)):
                        w = w.rearrange("(k p) i -> p k i", p=P)
                        whole, rest = m * FULL * P, 2 * FULL * P + m * REST
                        sp.dma_start(ffn_sb[:, :, whole:whole + FULL * P], w[:, :, 0:FULL * P])\
                          .then_inc(ffn_loaded, 16)
                        sp.dma_start(ffn_sb[:, :, rest:rest + REST], w[:, :, FULL * P:]).then_inc(ffn_loaded, 16)
                elif name == "down":
                    sp.dma_start(gbds[:, :], down_s.partition_broadcast(P)).then_inc(down_loaded, 16)
                    sp.dma_start(down_sb[:, 0:FULL, :],
                                 downT[0:FULL * P, :].rearrange("(j p) d -> p j d", p=P)).then_inc(down_loaded, 16)
                    sp.dma_start(down_sb[REST:P, FULL, :], downT[FULL * P:, :]).then_inc(down_loaded, 16)

            load_x(0)
            sp.dma_start(xproj_sb[:, :, :], xprojT.rearrange("(k p) e -> p k e", p=P)).then_inc(proj_loaded, 16)
            sp.dma_start(dtproj_sb[:, :], dtprojT).then_inc(proj_loaded, 16)
            for step in steps:
                for slot in range(N):
                    for kind, name, c in side_tasks("sync", step, slot):
                        if kind == "S":
                            load_more(name)
                        elif kind == "B" and name == "0":
                            load_brow(0)
                        elif kind == "B":
                            g = int(name)
                            if g < N // GROUP:
                                load_brow(step * (N // GROUP) + g)
                            elif step + 1 < NCH:
                                load_brow((step + 1) * (N // GROUP))
                        elif kind == "F":
                            sp.wait_ge(*emptied(("F bT", c, 0)))
                            sp.dma_start(bT_dram[:, TOK0[c]:TOK0[c] + CHUNK[c]], bT_sb[:, 0:CHUNK[c]])\
                              .then_inc(bT_stored, 16)
                        elif kind == "K":
                            q = int(name[-1])
                            sp.wait_ge(*emptied(("K down", c, q)))
                            b = BLK0[c] + 2 * q
                            sp.dma_start(out_dram[:, b:b + 2, :], resid[:, b:b + 2, :]).then_inc(out_stored, 16)
            sp.wait_ge(out_stored, 16 * sum(NPAIR))

        @block.gpsimd
        def _(pool):
            nc.gpsimd.memset(ident[:, :], 0.0).then_inc(ident_ready, 1)
            nc.gpsimd.memset(minus_half[:, :], -0.5).then_inc(minus_half_ready, 1)
            pool.wait_ge(ident_ready, 1)
            nc.gpsimd.affine_select(out=ident[:, :], in_=ident[:, :], compare_op=ALU.not_equal, fill=1.0,
                                    base=0, pattern=[[-1, P]], channel_multiplier=1).then_inc(ident_ready, 1)
            pool.wait_ge(minus_half_ready, 1)
            nc.gpsimd.memset(ones[:, :], 1.0).then_inc(ones_ready, 1)

            def side_work(kind, name, c):
                nb, S = NBLK[c], CHUNK[c]
                if kind == "S":
                    pool.wait_ge(down_loaded, 48)
                    pool.wait_ge(gbds_ready, 1)
                    nc.gpsimd.tensor_tensor(down_sb[:, 0:FULL, :], down_sb[:, 0:FULL, :],
                                            gbds[:, :].unsqueeze(1).to_broadcast([P, FULL, D]),
                                            ALU.mult).then_inc(down_scaled, 1)
                    pool.wait_ge(down_scaled, 1)
                    nc.gpsimd.tensor_tensor(down_sb[REST:P, FULL, :], down_sb[REST:P, FULL, :],
                                            gbds[REST:P, :], ALU.mult).then_inc(down_scaled, 1)
                    pool.wait_ge(down_scaled, 2)
                elif name == "lo":
                    low_part(pool, c)
                elif name == "rstd":
                    pool.wait_ge(meanvar_ready[kind], c + 1)
                    nc.gpsimd.tensor_scalar(vareps[kind][:, 0:nb], meanvar[kind][:, 0:nb, 1], EPS, 1.0,
                                            ALU.add, ALU.mult).then_inc(vareps_ready[kind], 1)
                    pool.wait_ge(vareps_ready[kind], c + 1)
                    nc.gpsimd.tensor_tensor(rstd[kind][:, 0:nb], vareps[kind][:, 0:nb], minus_half[:, 0:nb],
                                            ALU.pow).then_inc(rstd_ready[kind], 1)

            def keep_last(c, n):
                pool.wait_ge(scan_done, upto_scan(c, n, HALVES - 1))
                nc.gpsimd.tensor_copy(last[:, n, :], state[(c * N + n) % RING_STATE][:, :, CHUNK[c] - 1])\
                  .then_inc(last_kept, 1)

            def add_product(c, n):
                m, nb = ACT_STATES.index(n), NBLK[c]
                if m:
                    pool.wait_ge(prod_ready, upto_prod(c, n))
                    if m > 1:
                        pool.wait_ge(acc2_ready, upto_acc2(c, ACT_STATES[m - 1]))
                    nc.gpsimd.tensor_tensor(acc2[:, 0:nb, :], acc2[:, 0:nb, :], prod[m % 2][:, 0:nb, :],
                                            ALU.add).then_inc(acc2_ready, 1)

            for step in steps:
                for n in range(N):
                    if 0 <= step < NCH:
                        c, S, j = step, CHUNK[step], step * N + n
                        if n == 0:
                            pool.wait_ge(u_ready, c + 1)
                        if n % GROUP == 0:
                            group = j // GROUP
                            pool.wait_ge(brow_loaded[group % RING_B], 16 * (group // RING_B + 1))
                        if j >= RING_STATE:
                            cb, nb_ = divmod(j - RING_STATE, N)
                            pool.wait_ge(stateT_ready, pair_no(cb, nb_, NPAIR[cb] - 1) + 1)
                            if cb < NCH - 1:
                                pool.wait_ge(last_kept, j - RING_STATE + 1)
                        b = brow[(j // GROUP) % RING_B][:, n % GROUP, 0:S]
                        nc.gpsimd.tensor_tensor(state[j % RING_STATE][:, :, 0:S], u[:, c % 2, :, 0:S],
                                                b.unsqueeze(1).to_broadcast([P, HALVES, S]),
                                                ALU.mult).then_inc(drive_ready, 1)
                    for c, m in lagged(step, n, KEEP_LAG):
                        if c < NCH - 1:
                            keep_last(c, m)
                    for c, m in lagged(step, n, SUM_LAG):
                        if m in ACT_STATES:
                            add_product(c, m)
                    for task in side_tasks("gpsimd", step, n):
                        side_work(*task)

        @block.scalar
        def _(act):
            act.dma_start(pack_sb[:, :], pack).then_inc(pack_loaded, 16)
            act.dma_start(wmod_sb[:, :, 0:3 * D], wmod_v[:, :, 0:3 * D]).then_inc(wmod_loaded, 16)
            nc.scalar.preload_act_table_set("natural_log_exp_and_others")
            act.wait_ge(pack_loaded, 16)
            nc.scalar.activation(sigc[:, :], pack_sb[:, COL_C:COL_C + HALVES], ACT.Exp, scale=-1.0)\
              .then_inc(expc_ready, 1)
            nc.scalar.activation(A[:, :], pack_sb[:, COL_ALOG:COL_ALOG + HALVES * N], ACT.Exp)\
              .then_inc(A_exp_ready, 1)

            def side_work(kind, name, c):
                S, nb = CHUNK[c], NBLK[c]
                if name[:2] == "hi":
                    k = int(name[2:])
                    act.wait_ge(ffn_loaded, 64)
                    nc.scalar.activation(ffn_hi[:, k, :], ffn_sb[:, k, :], ACT.Copy).then_inc(ffn_hi_ready, 1)
                elif name[:4] == "same":
                    k = int(name[4:])
                    act.wait_ge(equal_ready, 1)
                    nc.scalar.activation(gates_flat[:, k, :], gates_flat[:, k, :], ACT.Copy,
                                         accum_out=same[:, k:k + 1]).then_inc(same_ready, 1)
                elif name[:2] == "xn":
                    q = int(name[2:])
                    act.wait_ge(nmr_ready[kind], c + 1)
                    for b in range(2 * q, 2 * q + 2):
                        ins = nc.scalar.activation(xn[kind][:, b, :], resid[:, BLK0[c] + b, :], ACT.Identity,
                                                   scale=rstd[kind][:, b:b + 1], bias=nmr[kind][:, b:b + 1])
                    ins.then_inc(xn_ready[kind], 1)
                elif name in ("hmod", "h2", "h2hi"):
                    if name == "hmod":
                        to, key, at = hmod, "F xT", 0
                        act.wait_ge(mod_steps, 1)
                        if c:
                            act.wait_ge(u_ready, c)
                            act.wait_ge(*emptied(("F dterm", c - 1, NPAIR[c - 1] - 1)))
                    else:
                        to, key, at = h2 if name == "h2" else h2_hi, "K h2T", 6
                        act.wait_ge(*emptied(("S mod2", 0, 0)))
                    for h in range(HALVES):
                        src, i, k = side_bank((key, c, h))
                        act.wait_ge(side_full[i], k + 1)
                        done = h2_hi_ready if name == "h2hi" else side_free[i]
                        nc.scalar.activation(to[:, h, 0:S], src[:, 0:S], ACT.Identity,
                                             scale=mod[:, at + 2 + h:at + 3 + h],
                                             bias=mod[:, at + h:at + h + 1]).then_inc(done, 1)
                elif kind == "F" and name in ("dt", "bT", "c"):
                    src, i, k = side_bank((f"F {name}", c, 0))
                    if name == "bT" and c:
                        act.wait_ge(bT_stored, 16 * c)
                    act.wait_ge(side_full[i], k + 1)
                    if name == "dt":
                        to, src = dt_sb[:, 0:S], src[:, 0:S]
                    elif name == "bT":
                        to, src = bT_sb[:, 0:S], src[0:N, 0:S]
                    else:
                        to, src = C_sb[:, c % 2, 0:nb, :], \
                            src[:, 0:nb * N].rearrange("p (b n) -> p b n", n=N)
                    nc.scalar.activation(to, src, ACT.Copy).then_inc(side_free[i], 1)
                elif name == "exp":
                    if c:
                        act.wait_ge(*emptied(("F z", c - 1, HALVES - 1)))
                    for h in range(HALVES):
                        src, i, k = side_bank(("F z", c, h))
                        act.wait_ge(side_full[i], k + 1)
                        nc.scalar.activation(splus[:, h, 0:S], src[:, 0:S], ACT.Exp,
                                             bias=pack_sb[:, COL_DTB + h:COL_DTB + h + 1]).then_inc(spexp_ready, 1)
                elif name == "ln":
                    act.wait_ge(spcap_ready, c + 1)
                    nc.scalar.activation(splus[:, :, 0:S], splus[:, :, 0:S], ACT.Ln, bias=1.0)\
                      .then_inc(spln_ready, 1)
                elif name[:4] == "gate":
                    j = int(name[4:])
                    src, i, k = side_bank((f"K {name}", c, 0))
                    act.wait_ge(side_full[i], k + 1)
                    nc.scalar.activation(gates[:, c % 2, j, 0:S], src[:, 0:S],
                                         ACT.Silu if c == NCH - 1 else ACT.Copy,
                                         scale=pack_sb[:, COL_GS + j:COL_GS + j + 1]).then_inc(side_free[i], 1)
                elif name == "mixed":
                    src, i, k = side_bank(("K mixed", c, 0))
                    act.wait_ge(side_full[i], k + 1)
                    nc.scalar.activation(gates[REST:P, c % 2, FULL, 0:S], src[0:REST, 0:S],
                                         ACT.Silu if c == NCH - 1 else ACT.Copy,
                                         scale=pack_sb[0:REST, COL_GS + FULL:COL_GS + FULL + 1])
                    nc.scalar.activation(up5[REST:P, 0:S], src[REST:P, 0:S], ACT.Copy,
                                         scale=pack_sb[REST:P, COL_GS + FULL:COL_GS + FULL + 1])\
                      .then_inc(side_free[i], 1)
                elif name == "silu":
                    for j in range(FULL):
                        act.wait_ge(*emptied((f"K gate{j}", c, 0)))
                    act.wait_ge(*emptied(("K mixed", c, 0)))
                    nc.scalar.activation(gates[:, c % 2, 0:FULL, 0:S], gates[:, c % 2, 0:FULL, 0:S], ACT.Silu)
                    rest = gates[REST:P, c % 2, FULL, 0:S]
                    nc.scalar.activation(rest, rest, ACT.Silu)\
                      .then_inc(silu_ready, 1)
                    nc.scalar.preload_act_table_set("natural_log_exp_and_others")

            def multiply(c, n):
                m = ACT_STATES.index(n)
                if m == 0:
                    act.wait_ge(*emptied(("F c", c, 0)))
                    if c:
                        act.wait_ge(acc2_added, c)
                elif m > 2:
                    act.wait_ge(acc2_ready, upto_acc2(c, ACT_STATES[m - 2]))
                elif c:
                    act.wait_ge(acc2_ready, upto_acc2(c - 1, ACT_STATES[-1]))
                for q in range(NPAIR[c]):
                    number = pair_no(c, n, q)
                    act.wait_ge(stateT_ready, number + 1)
                    for b in range(2):
                        ins = nc.scalar.activation((prod[m % 2] if m else acc2)[:, 2 * q + b, :],
                                                   stateT[number % RING_HT][:, b * D:(b + 1) * D], ACT.Copy,
                                                   scale=C_sb[:, c % 2, 2 * q + b, n:n + 1])
                    ins.then_inc(prod_ready, 1)

            for step in steps:
                if step == 0:
                    act.wait_ge(A_ready, 1)
                for n in range(N):
                    if 0 <= step < NCH:
                        c, S = step, CHUNK[step]
                        if n == 0:
                            act.wait_ge(*emptied(("F z", c, HALVES - 1)))
                        for h in range(HALVES):
                            i = upto_scan(c, n, h) - 1
                            if i >= RING_DECAY:
                                act.wait_ge(scan_done, i - RING_DECAY + 1)
                            nc.scalar.activation(decay[i % RING_DECAY][:, 0:S], delta[:, c % 2, h, 0:S], ACT.Exp,
                                                 scale=A[:, h * N + n:h * N + n + 1]).then_inc(decay_ready, 1)
                    for c, m in lagged(step, n, MUL_LAG):
                        if m in ACT_STATES:
                            multiply(c, m)
                    for task in side_tasks("scalar", step, n):
                        side_work(*task)

        @block.vector
        def _(dve):
            dve.wait_ge(expc_ready, 1)
            nc.vector.tensor_scalar(sigc[:, :], sigc[:, :], 1.0, None, ALU.add).then_inc(silc_steps, 1)
            dve.wait_ge(silc_steps, 1)
            nc.vector.reciprocal(sigc[:, :], sigc[:, :]).then_inc(silc_steps, 1)
            dve.wait_ge(silc_steps, 2)
            nc.vector.tensor_tensor(silc[:, :], sigc[:, :], pack_sb[:, COL_C:COL_C + HALVES], ALU.mult)\
              .then_inc(silc_steps, 1)
            dve.wait_ge(silc_steps, 3)
            nc.vector.tensor_copy(silc_wide[:, :, :], silc[:, :].unsqueeze(2).to_broadcast([P, HALVES, P]))\
              .then_inc(silc_steps, 1)
            dve.wait_ge(A_exp_ready, 1)
            nc.vector.tensor_scalar(A[:, :], A[:, :], -1.0, None, ALU.mult).then_inc(A_ready, 1)

            def ln_stats(kind, c):
                for b in range(NBLK[c]):
                    ins = nc.vector.bn_stats(stats[kind][:, b, :], resid[:, BLK0[c] + b, :])
                ins.then_inc(stats_ready[kind], 1)
                dve.wait_ge(stats_ready[kind], c + 1)
                for b in range(NBLK[c]):
                    ins = nc.vector.bn_aggr(meanvar[kind][:, b, :], stats[kind][:, b, :])
                ins.then_inc(meanvar_ready[kind], 1)

            def side_work(kind, name, c):
                S, nb = CHUNK[c], NBLK[c]
                if name == "stats":
                    if kind == "F":
                        dve.wait_ge(x_loaded[c], 16)
                    else:
                        dve.wait_ge(acc2_added, c + 1)
                    ln_stats(kind, c)
                elif name == "acc2":
                    m = ACT_STATES[-1]
                    dve.wait_ge(acc2_ready, upto_acc2(c, m))
                    dve.wait_ge(acc_done, upto_acc(c, N - 1, nb - 1))
                    to = resid[:, BLK0[c]:BLK0[c] + nb, :]
                    nc.vector.tensor_tensor(to, to, acc2[:, 0:nb, :], ALU.add).then_inc(acc2_added, 1)
                elif name == "h2":
                    dve.wait_ge(*emptied(("S mod2", 0, 0)))
                    for h in range(HALVES):
                        src, i, k = side_bank(("K h2T", c, h))
                        dve.wait_ge(side_full[i], k + 1)
                        dve.wait_ge(h2_hi_ready, HALVES * c + h + 1)
                        nc.vector.tensor_scalar(h2[:, h, 0:S], src[:, 0:S], mod[:, 8 + h:9 + h], mod[:, 6 + h:7 + h],
                                                ALU.mult, ALU.add).then_inc(side_free[i], 1)
                elif name == "lo":
                    low_part(dve, c)
                elif name == "nmr":
                    dve.wait_ge(rstd_ready[kind], c + 1)
                    nc.vector.scalar_tensor_tensor(nmr[kind][:, 0:nb], meanvar[kind][:, 0:nb, 0], -1.0,
                                                   rstd[kind][:, 0:nb], ALU.mult, ALU.mult)\
                      .then_inc(nmr_ready[kind], 1)
                elif name == "cap":
                    dve.wait_ge(spexp_ready, HALVES * (c + 1))
                    nc.vector.tensor_scalar(splus[:, :, 0:S], splus[:, :, 0:S], EXP_CAP, None, ALU.min)\
                      .then_inc(spcap_ready, 1)
                elif name == "delta":
                    dve.wait_ge(spln_ready, c + 1)
                    for h in range(HALVES):
                        src, i, k = side_bank(("F z", c, h))
                        dve.wait_ge(side_full[i], k + 1)
                        nc.vector.scalar_tensor_tensor(delta[:, c % 2, h, 0:S], src[:, 0:S],
                                                       pack_sb[:, COL_DTB + h:COL_DTB + h + 1],
                                                       splus[:, h, 0:S], ALU.add, ALU.max)\
                          .then_inc(side_free[i], 1)
                    dve.wait_ge(side_free[i], k + 1)
                    dve.wait_ge(*emptied(("F xT", c, HALVES - 1)))
                    for h in range(HALVES):
                        ins = nc.vector.scalar_tensor_tensor(u[:, c % 2, h, 0:S], delta[:, c % 2, h, 0:S],
                                                             ga[:, h:h + 1], hmod[:, h, 0:S],
                                                             ALU.mult, ALU.mult)
                    ins.then_inc(u_ready, 1)
                elif name == "dterm":
                    for q in range(NPAIR[c]):
                        src, i, k = side_bank(("F dterm", c, q))
                        dve.wait_ge(side_full[i], k + 1)
                        b = BLK0[c] + 2 * q
                        nc.vector.tensor_tensor(resid[:, b:b + 2, :], resid[:, b:b + 2, :],
                                                src[:, :].rearrange("p (b d) -> p b d", b=2), ALU.add)\
                          .then_inc(side_free[i], 1)
                elif name == "hdn5":
                    if c < NCH - 1:
                        dve.wait_ge(silu_ready, c + 1)
                    dve.wait_ge(*emptied(("K mixed", c, 0)))
                    g = gates[REST:P, c % 2, FULL, 0:CHUNK[c]]
                    nc.vector.tensor_tensor(g, g, up5[REST:P, 0:CHUNK[c]], ALU.mult).then_inc(hdn5_ready, 1)
                elif name[:3] == "hdn":
                    j = int(name[3:])
                    src, i, k = side_bank((f"K up{j}", c, 0))
                    if c < NCH - 1:
                        dve.wait_ge(silu_ready, c + 1)
                    else:
                        dve.wait_ge(*emptied((f"K gate{j}", c, 0)))
                    dve.wait_ge(side_full[i], k + 1)
                    nc.vector.scalar_tensor_tensor(gates[:, c % 2, j, 0:S], src[:, 0:S],
                                                   pack_sb[:, COL_US + j:COL_US + j + 1], gates[:, c % 2, j, 0:S],
                                                   ALU.mult, ALU.mult).then_inc(side_free[i], 1)
                elif name[:3] == "out":
                    q = int(name[3:])
                    src, i, k = side_bank(("K down", c, q))
                    dve.wait_ge(side_full[i], k + 1)
                    b = BLK0[c] + 2 * q
                    nc.vector.tensor_tensor(resid[:, b:b + 2, :], resid[:, b:b + 2, :],
                                            src[:, :].rearrange("p (b d) -> p b d", b=2), ALU.add)\
                      .then_inc(side_free[i], 1)

            def add_state(c, n):
                for b in range(NBLK[c]):
                    number = pair_no(c, n, b // 2)
                    if b % 2 == 0:
                        dve.wait_ge(stateT_ready, number + 1)
                    if dve_states(n) > 1:
                        dve.wait_ge(acc_done, upto_acc(c, n, b) - NBLK[c])
                    elif b == 0:
                        dve.wait_ge(*emptied(("F c", c, 0)))
                        dve.wait_ge(*emptied(("F dterm", c, NPAIR[c] - 1)))
                    row = resid[:, BLK0[c] + b, :]
                    nc.vector.scalar_tensor_tensor(row, stateT[number % RING_HT][:, (b % 2) * D:(b % 2 + 1) * D],
                                                   C_sb[:, c % 2, b, n:n + 1], row, ALU.mult, ALU.add)\
                      .then_inc(acc_done, 1)

            clamp_count = [0]

            def clamp_gate(sign, to, gate, use=None):
                def link(ins):
                    clamp_count[0] += 1
                    ins.then_inc(clamp_steps, 1)
                    dve.wait_ge(clamp_steps, clamp_count[0])

                link(nc.vector.tensor_scalar(sign[:, :], gate, 0.0, 2.0, ALU.is_ge, ALU.mult))
                link(nc.vector.tensor_scalar(sign[:, :], sign[:, :], -1.0, None, ALU.add))
                link(nc.vector.tensor_tensor(to[:, :], gate, sign[:, :], ALU.mult))
                ins = nc.vector.scalar_tensor_tensor(to[:, :], to[:, :], 0.25, sign[:, :], ALU.max, ALU.mult)
                if use is None:
                    link(ins)
                else:
                    ins.then_inc(emptied(use)[0], 1)
                    dve.wait_ge(*emptied(use))

            def setup(name):
                if name == "mod":
                    src, i, k = side_bank(("S mod", 0, 0))
                    dve.wait_ge(side_full[i], k + 1)
                    nc.vector.tensor_copy(mod[:, 0:6], src[:, 0:6]).then_inc(side_free[i], 1)
                    dve.wait_ge(side_free[i], k + 1)
                    nc.vector.tensor_scalar(mod[:, 2:4], mod[:, 2:4], 1.0, None, ALU.add).then_inc(mod_steps, 1)
                    clamp_gate(sgn, ga, mod[:, 4:6])
                    nc.vector.tensor_tensor(gaD[:, :], ga[:, :], pack_sb[:, COL_D:COL_D + HALVES], ALU.mult)\
                      .then_inc(mod_steps, 1)
                    dve.wait_ge(mod_steps, 2)
                    dve.wait_ge(ident_ready, 2)
                    for h in range(HALVES):
                        ins = nc.vector.tensor_scalar(diag_gaD[:, h, :], ident[:, :], gaD[:, h:h + 1], None,
                                                      ALU.mult)
                    ins.then_inc(mod_steps, 1)
                elif name == "mod2":
                    src, i, k = side_bank(("S mod2", 0, 0))
                    dve.wait_ge(side_full[i], k + 1)
                    nc.vector.tensor_copy(mod[:, 6:8], src[:, 0:2])
                    nc.vector.tensor_scalar(mod[:, 8:10], src[:, 2:4], 1.0, None, ALU.add)\
                      .then_inc(side_free[i], 1)
                elif name == "gb":
                    src, i, k = side_bank(("S gb", 0, 0))
                    dve.wait_ge(side_full[i], k + 1)
                    clamp_gate(row_sgn, row_abs, src[:, 0:D], ("S gb", 0, 0))
                    dve.wait_ge(down_loaded, 48)
                    nc.vector.tensor_tensor(gbds[:, :], gbds[:, :], row_abs[:, :], ALU.mult)\
                      .then_inc(gbds_ready, 1)
                elif name == "equal":
                    dve.wait_ge(ffn_hi_ready, HALVES)
                    nc.vector.tensor_tensor(gates_flat, ffn_hi[:, :, :].bitcast(F32), ffn_sb[:, :, :],
                                            ALU.is_equal).then_inc(equal_ready, 1)
                elif name == "same":
                    src, i, k = side_bank(("S same", 0, 0))
                    dve.wait_ge(side_full[i], k + 1)
                    weights = P * HALVES * 2 * INTER
                    nc.vector.tensor_scalar(needs_full[:, :], src[0:1, 0:1], weights - 0.5, None, ALU.is_lt)\
                      .then_inc(side_free[i], 1)

            for step in steps:
                for n in range(N):
                    if 0 <= step < NCH:
                        c, S = step, CHUNK[step]
                        for h in range(HALVES):
                            i = upto_scan(c, n, h) - 1
                            dve.wait_ge(decay_ready, i + 1)
                            if h == 0:
                                dve.wait_ge(drive_ready, upto_drive(c, n))
                            if c and h == 0:
                                dve.wait_ge(last_kept, (c - 1) * N + n + 1)
                            before = last[:, n, h:h + 1] if c else 0.0
                            to = state[(c * N + n) % RING_STATE][:, h, 0:S]
                            nc.vector.tensor_tensor_scan(to, decay[i % RING_DECAY][:, 0:S], to, before,
                                                         ALU.mult, ALU.add).then_inc(scan_done, 1)
                        if n and n - 1 not in ACT_STATES:
                            add_state(c, n - 1)
                        elif n == 0 and c:
                            add_state(c - 1, N - 1)
                    elif step == NCH and n == 0:
                        add_state(NCH - 1, N - 1)
                    for task in side_tasks("vector", step, n):
                        if task[0] == "S":
                            setup(task[1])
                        else:
                            side_work(*task)

        @block.tensor
        def _(pe):
            def take(use):
                to, i, k = side_bank(use)
                if k:
                    pe.wait_ge(side_free[i], k)
                return to, side_full[i]

            pe.wait_ge(ident_ready, 2)
            for _ in range(WARM_UP):
                nc.tensor.transpose(stateT[0][:, 0:P], ident[:, :], ident[:, :])

            def setup(name):
                if name == "warm":
                    for _ in range(KEEP_WARM):
                        nc.tensor.transpose(stateT[0][:, 0:P], ident[:, :], ident[:, :])
                    return
                to, full = take((f"S {name}", 0, 0))
                if name in ("mod", "mod2"):
                    pe.wait_ge(silc_steps, 3)
                    pe.wait_ge(wmod_loaded if name == "mod" else wmod2_loaded, 16)
                    first, cols = (0, 6) if name == "mod" else (6, 4)
                    for col in range(cols):
                        for k in range(HALVES):
                            ins = nc.tensor.matmul(to[:, col:col + 1],
                                                   wmod_sb[:, k, (first + col) * P:(first + col + 1) * P],
                                                   silc[:, k:k + 1], start=k == 0, stop=k == HALVES - 1)
                elif name == "gb":
                    pe.wait_ge(silc_steps, 4)
                    pe.wait_ge(wmod2_loaded, 16)
                    for k in range(HALVES):
                        ins = nc.tensor.matmul(to[:, 0:D], silc_wide[:, k, :], wmod_sb[:, k, 5 * D:6 * D],
                                               start=k == 0, stop=k == HALVES - 1)
                elif name == "same":
                    pe.wait_ge(ones_ready, 1)
                    pe.wait_ge(same_ready, HALVES)
                    for k in range(HALVES):
                        ins = nc.tensor.matmul(to[0:1, 0:1], same[:, k:k + 1], ones[:, :], start=k == 0,
                                               stop=k == HALVES - 1)
                ins.then_inc(full, 1)

            def product(use, S, M, weights, data):
                to, full = take(use)
                for k in range(HALVES):
                    ins = nc.tensor.matmul(to[0:M, 0:S], weights(k), data(k), start=k == 0, stop=k == HALVES - 1)
                ins.then_inc(full, 1)

            def side_work(kind, name, c, full_weights):
                S, nb = CHUNK[c], NBLK[c]
                if kind == "S":
                    setup(name)
                elif name in ("xT", "h2T"):
                    if c == 0:
                        pe.wait_ge(ident_ready, 2)
                    pe.wait_ge(xn_ready[kind], PAIR0[c] + NPAIR[c])
                    for h in range(HALVES):
                        to, full = take((f"{kind} {name}", c, h))
                        for b in range(nb):
                            ins = nc.tensor.transpose(to[:, b * P:(b + 1) * P],
                                                      xn[kind][:, b, h * P:(h + 1) * P], ident[:, :])
                        ins.then_inc(full, 1)
                elif name == "dt":
                    pe.wait_ge(proj_loaded, 32)
                    pe.wait_ge(*emptied(("F xT", c, HALVES - 1)))
                    product(("F dt", c, 0), S, R, lambda k: xproj_sb[:, k, 0:R], lambda k: hmod[:, k, 0:S])
                elif name == "bT":
                    pe.wait_ge(proj_loaded, 32)
                    pe.wait_ge(*emptied(("F xT", c, HALVES - 1)))
                    product(("F bT", c, 0), S, N, lambda k: xproj_sb[:, k, R:R + N], lambda k: hmod[:, k, 0:S])
                elif name == "c":
                    to, full = take(("F c", c, 0))
                    for b in range(nb):
                        for k in range(HALVES):
                            ins = nc.tensor.matmul(to[:, b * N:(b + 1) * N], hmod[:, k, b * P:(b + 1) * P],
                                                   xproj_sb[:, k, R + N:R + 2 * N],
                                                   start=k == 0, stop=k == HALVES - 1)
                    ins.then_inc(full, 1)
                elif name == "z":
                    pe.wait_ge(*emptied(("F dt", c, 0)))
                    for h in range(HALVES):
                        to, full = take(("F z", c, h))
                        nc.tensor.matmul(to[:, 0:S], dtproj_sb[:, h * P:(h + 1) * P], dt_sb[:, 0:S],
                                         start=True, stop=True).then_inc(full, 1)
                elif name == "dterm":
                    pe.wait_ge(mod_steps, 3)
                    for q in range(NPAIR[c]):
                        to, full = take(("F dterm", c, q))
                        for b in range(2):
                            for h in range(HALVES):
                                ins = nc.tensor.matmul(to[:, b * D + h * P:b * D + (h + 1) * P],
                                                       hmod[:, h, (2 * q + b) * P:(2 * q + b + 1) * P],
                                                       diag_gaD[:, h, :], start=True, stop=True)
                        ins.then_inc(full, 1)
                elif name == "mixed" or name[:4] == "gate" or name[:2] == "up":
                    j = 2 * FULL if name == "mixed" else int(name[4:]) if name[0] == "g" else FULL + int(name[2:])
                    tile = slice(j * P, (j + 1) * P)
                    if full_weights:
                        pe.wait_ge(*emptied(("K h2T", c, HALVES - 1)))
                        product((f"K {name}", c, 0), S, P, lambda k: ffn_sb[:, k, tile], lambda k: h2[:, k, 0:S])
                    else:
                        pe.wait_ge(h2_hi_ready, HALVES * (c + 1))
                        to, full = take((f"K {name}", c, 0))
                        for part in (h2_hi, h2_lo):
                            if part is h2_lo:
                                pe.wait_ge(h2_lo_ready, c + 1)
                            for k in range(HALVES):
                                ins = nc.tensor.matmul(to[:, 0:S], ffn_hi[:, k, tile], part[:, k, 0:S],
                                                       start=part is h2_hi and k == 0,
                                                       stop=part is h2_lo and k == HALVES - 1)
                        ins.then_inc(full, 1)
                elif name[:4] == "down" and c == NCH - 1:
                    pair = int(name[4:]) // 2
                    pe.wait_ge(down_scaled, 2)
                    to, full = take(("K down", c, pair))
                    for j in (FULL, *range(FULL)):
                        part = slice(REST, P) if j == FULL else slice(0, P)
                        if j == FULL:
                            pe.wait_ge(hdn5_ready, c + 1)
                        else:
                            pe.wait_ge(*emptied((f"K up{j}", c, 0)))
                        for b in range(2):
                            rows = slice((2 * pair + b) * P, (2 * pair + b + 1) * P)
                            ins = nc.tensor.matmul(to[:, b * D:(b + 1) * D], gates[part, c % 2, j, rows],
                                                   down_sb[part, j, :], start=j == FULL and b == 0,
                                                   stop=j == FULL - 1 and b == 1)
                    ins.then_inc(full, 1)
                elif name[:4] == "down":
                    b = int(name[4:])
                    if b == 0:
                        pe.wait_ge(down_scaled, 2)
                        pe.wait_ge(*emptied((f"K up{FULL - 1}", c, 0)))
                        pe.wait_ge(hdn5_ready, c + 1)
                    to, i, k = side_bank(("K down", c, b // 2))
                    if b % 2 == 0 and k:
                        pe.wait_ge(side_free[i], k)
                    rows = slice(b * P, (b + 1) * P)
                    to = to[:, (b % 2) * D:(b % 2 + 1) * D]
                    for j in range(FULL):
                        nc.tensor.matmul(to, gates[:, c % 2, j, rows], down_sb[:, j, :], start=j == 0, stop=False)
                    ins = nc.tensor.matmul(to, gates[REST:P, c % 2, FULL, rows], down_sb[REST:P, FULL, :],
                                           start=False, stop=True)
                    if b % 2:
                        ins.then_inc(side_full[i], 1)

            def run_step(step, full_weights):
                for n in range(N):
                    if 0 <= step < NCH:
                        c = step
                        pe.wait_ge(scan_done, upto_scan(c, n, HALVES - 1))
                        of = state[(c * N + n) % RING_STATE]
                        for q in range(NPAIR[c]):
                            number = pair_no(c, n, q)
                            if number >= RING_HT:
                                pe.wait_ge(*pair_read(*PAIRS[number - RING_HT]))
                            to = stateT[number % RING_HT]
                            for b in range(2):
                                for h in range(HALVES):
                                    ins = nc.tensor.transpose(
                                        to[:, b * D + h * P:b * D + (h + 1) * P],
                                        of[:, h, (2 * q + b) * P:(2 * q + b + 1) * P], ident[:, :])
                            ins.then_inc(stateT_ready, 1)
                    for task in side_tasks("tensor", step, n):
                        side_work(*task, full_weights)

            run_step(FIRST_F, True)
            run_step(0, True)
            pe.wait_ge(*emptied(("S same", 0, 0)))
            flag = pe.value_load(needs_full[0:1, 0:1], min_val=0, max_val=1)
            with pe.If(flag == 0):
                for step in range(1, LAST + 1):
                    run_step(step, False)
            with pe.Else():
                for step in range(1, LAST + 1):
                    run_step(step, True)



def kernel(L0_attn_x, L0_attn_A_log, L0_attn_D_param, L0_attn_x_proj_w, L0_attn_dt_proj_w, L0_attn_dt_proj_b,
           L0_ffn_gate_w, L0_ffn_up_w, L0_ffn_down_w, L0_ffn_gate_s, L0_ffn_up_s, L0_ffn_down_s, L0_c, L0_wmod):
    import numpy as np
    import concourse.bacc as bacc
    from concourse.bass_utils import run_bass_kernel_spmd

    def cols(v):
        return np.asarray(v).reshape(-1, P).T

    gate_s, up_s = np.asarray(L0_ffn_gate_s), np.asarray(L0_ffn_up_s)
    whole = FULL * P
    pack = np.concatenate([
        np.asarray(L0_attn_A_log).reshape(HALVES, P, N).transpose(1, 0, 2).reshape(P, HALVES * N),
        cols(L0_attn_D_param), cols(L0_attn_dt_proj_b),
        cols(gate_s[:whole]), np.concatenate([gate_s[whole:], up_s[whole:]])[:, None], cols(up_s[:whole]),
        cols(np.asarray(L0_c)[0]),
    ], axis=1)
    arrays = {
        "x": np.asarray(L0_attn_x)[0],
        "wmod": np.asarray(L0_wmod),
        "pack": pack,
        "down_s": np.asarray(L0_ffn_down_s),
        "xprojT": np.asarray(L0_attn_x_proj_w).T,
        "dtprojT": np.asarray(L0_attn_dt_proj_w).T,
        "gateT": np.asarray(L0_ffn_gate_w).T,
        "upT": np.asarray(L0_ffn_up_w).T,
        "downT": np.asarray(L0_ffn_down_w).T,
    }
    arrays = {k: np.ascontiguousarray(v) for k, v in arrays.items()}
    nc = bacc.Bacc("TRN2", target_bir_lowering=False, num_devices=1)
    args = [nc.dram_tensor(f"in_{k}", v.shape, mybir.dt.from_np(v.dtype), kind="ExternalInput").ap()
            for k, v in arrays.items()]
    out = nc.dram_tensor("out_0", (T, D), F32, kind="ExternalOutput").ap()
    adaln_block(nc, *args, out)
    r = run_bass_kernel_spmd(nc, [{f"in_{k}": v for k, v in arrays.items()}], core_ids=[0])
    return r.results[0]["out_0"].reshape(1, T, D)
```
